# Optimizing a Trainium2 kernel written in Bass

```python
import numpy as np
import jax
import jax.numpy as jnp

def _softmax(x, axis=-1):
    return jax.nn.softmax(x, axis=axis)

def _gelu(x):
    return jax.nn.gelu(x, approximate=True)

def _silu(x):
    return jax.nn.silu(x)

def _sigmoid(x):
    return jax.nn.sigmoid(x)

def _layernorm(x, axis=-1, eps=1e-05):
    m = jnp.mean(x, axis=axis, keepdims=True)
    v = jnp.var(x, axis=axis, keepdims=True)
    return (x - m) / jnp.sqrt(v + eps)

def _scatter_add(tgt, idx, src, axis=0):
    return tgt.at[idx].add(src)

def _segment_sum(src, seg, n):
    return jax.ops.segment_sum(src, seg, n)
kernel_name = 'mk_cond_seq_d1_seqx_r2_7b0f0c'

def setup_inputs(seed: int=0):
    np.random.seed(seed)
    _w = jnp.asarray

    def _rec_inputs():
        import jax
        import jax.numpy as jnp
        _rk = jax.random.key(seed)
        x = 7.22e-05 + 1 * jax.random.normal(jax.random.fold_in(_rk, 1), (2, 2048, 512), jnp.float32)
        _lenS = 2048 - jax.random.randint(jax.random.fold_in(_rk, 7), (2,), 0, max(1, 2048 // 4) + 1, jnp.int32)
        _lenS2 = 2048 - jax.random.randint(jax.random.fold_in(_rk, 8), (2,), 0, max(1, 2048 // 4) + 1, jnp.int32)
        cond_1024 = 0.00782532 + 1.00527 * jax.random.normal(jax.random.fold_in(_rk, 11), (2, 512), jnp.float32)
        return (x, cond_1024)
    x, cond_1024 = _rec_inputs()

    def _L0_cond_setup():
        import jax, jax.numpy as jnp
        import numpy as np
        D = 512
        H = 16
        HD = D // H
        FF = 4 * D
        LN_EPS = 1e-05

        def _layernorm(x, w, b):
            mu = jnp.mean(x, axis=-1, keepdims=True)
            var = jnp.mean(jnp.square(x - mu), axis=-1, keepdims=True)
            return (x - mu) * jax.lax.rsqrt(var + LN_EPS) * w + b
        key = jax.random.key(seed)
        ks = jax.random.split(key, 12)
        s = 0.02
        return {'x': jax.random.normal(ks[0], (8, 512, D), jnp.float32), 'c': jax.random.normal(ks[1], (8, D), jnp.float32), 'ln1_w': jnp.ones((D,), jnp.float32), 'ln1_b': jnp.zeros((D,), jnp.float32), 'ln2_w': jnp.ones((D,), jnp.float32), 'ln2_b': jnp.zeros((D,), jnp.float32), 'ada_w': jax.random.normal(ks[2], (D, 6 * D), jnp.float32) * s, 'ada_b': jnp.zeros((6 * D,), jnp.float32), 'qkv_w': jax.random.normal(ks[3], (D, 3 * D), jnp.float32) * s, 'qkv_b': jnp.zeros((3 * D,), jnp.float32), 'proj_w': jax.random.normal(ks[4], (D, D), jnp.float32) * s, 'proj_b': jnp.zeros((D,), jnp.float32), 'fc1_w': jax.random.normal(ks[5], (D, FF), jnp.float32) * s, 'fc1_b': jnp.zeros((FF,), jnp.float32), 'fc2_w': jax.random.normal(ks[6], (FF, D), jnp.float32) * s, 'fc2_b': jnp.zeros((D,), jnp.float32)}
    _L0_cond_all = _L0_cond_setup()
    _L0_cond_in = {k: v for k, v in _L0_cond_all.items() if k in ('ln1_w', 'ln1_b', 'ln2_w', 'ln2_b', 'ada_w', 'ada_b', 'qkv_w', 'qkv_b', 'proj_w', 'proj_b', 'fc1_w', 'fc1_b', 'fc2_w', 'fc2_b')}
    del _L0_cond_all
    return {'x': x, 'cond_1024': cond_1024, 'L0_cond_ln1_w': _L0_cond_in['ln1_w'], 'L0_cond_ln1_b': _L0_cond_in['ln1_b'], 'L0_cond_ln2_w': _L0_cond_in['ln2_w'], 'L0_cond_ln2_b': _L0_cond_in['ln2_b'], 'L0_cond_ada_w': _L0_cond_in['ada_w'], 'L0_cond_ada_b': _L0_cond_in['ada_b'], 'L0_cond_qkv_w': _L0_cond_in['qkv_w'], 'L0_cond_qkv_b': _L0_cond_in['qkv_b'], 'L0_cond_proj_w': _L0_cond_in['proj_w'], 'L0_cond_proj_b': _L0_cond_in['proj_b'], 'L0_cond_fc1_w': _L0_cond_in['fc1_w'], 'L0_cond_fc1_b': _L0_cond_in['fc1_b'], 'L0_cond_fc2_w': _L0_cond_in['fc2_w'], 'L0_cond_fc2_b': _L0_cond_in['fc2_b']}

def reference(x, cond_1024, L0_cond_ln1_w, L0_cond_ln1_b, L0_cond_ln2_w, L0_cond_ln2_b, L0_cond_ada_w, L0_cond_ada_b, L0_cond_qkv_w, L0_cond_qkv_b, L0_cond_proj_w, L0_cond_proj_b, L0_cond_fc1_w, L0_cond_fc1_b, L0_cond_fc2_w, L0_cond_fc2_b):
    import jax
    import jax.numpy as jnp

    def _L0_cond_ref(x, c, ln1_w, ln1_b, ln2_w, ln2_b, ada_w, ada_b, qkv_w, qkv_b, proj_w, proj_b, fc1_w, fc1_b, fc2_w, fc2_b):
        import jax, jax.numpy as jnp
        import numpy as np
        D = 512
        H = 16
        HD = D // H
        FF = 4 * D
        LN_EPS = 1e-05

        def _layernorm(x, w, b):
            mu = jnp.mean(x, axis=-1, keepdims=True)
            var = jnp.mean(jnp.square(x - mu), axis=-1, keepdims=True)
            return (x - mu) * jax.lax.rsqrt(var + LN_EPS) * w + b
        B, L, _ = x.shape
        ssg = jax.nn.silu(c) @ ada_w + ada_b
        msa_shift, msa_scale, msa_gate, mlp_shift, mlp_scale, mlp_gate = jnp.split(ssg, 6, axis=-1)

        def modulate(h, shift, scale):
            return h * (1.0 + scale[:, None, :]) + shift[:, None, :]
        h = modulate(_layernorm(x, ln1_w, ln1_b), msa_shift, msa_scale)
        qkv = h @ qkv_w + qkv_b
        q, k, v = jnp.split(qkv, 3, axis=-1)
        q = q.reshape(B, L, H, HD).transpose(0, 2, 1, 3)
        k = k.reshape(B, L, H, HD).transpose(0, 2, 1, 3)
        v = v.reshape(B, L, H, HD).transpose(0, 2, 1, 3)
        scores = jnp.einsum('bhqd,bhkd->bhqk', q, k) / jnp.sqrt(jnp.float32(HD))
        attn = jax.nn.softmax(scores, axis=-1)
        a = jnp.einsum('bhqk,bhkd->bhqd', attn, v)
        a = a.transpose(0, 2, 1, 3).reshape(B, L, D)
        a = a @ proj_w + proj_b
        x = x + msa_gate[:, None, :] * a
        h = modulate(_layernorm(x, ln2_w, ln2_b), mlp_shift, mlp_scale)
        h = jax.nn.gelu(h @ fc1_w + fc1_b, approximate=True)
        h = h @ fc2_w + fc2_b
        x = x + mlp_gate[:, None, :] * h
        return x
    x = _L0_cond_ref(x, cond_1024, L0_cond_ln1_w, L0_cond_ln1_b, L0_cond_ln2_w, L0_cond_ln2_b, L0_cond_ada_w, L0_cond_ada_b, L0_cond_qkv_w, L0_cond_qkv_b, L0_cond_proj_w, L0_cond_proj_b, L0_cond_fc1_w, L0_cond_fc1_b, L0_cond_fc2_w, L0_cond_fc2_b)
    return x

_drawn_inputs = setup_inputs


def setup_inputs(seed=0):
    import zlib

    import numpy as np

    out = dict(_drawn_inputs(seed))
    spreads = {'L0_cond_ln1_w': (1.0, 0.6),
     'L0_cond_ln1_b': (0.0, 0.8),
     'L0_cond_ln2_w': (1.0, 0.6),
     'L0_cond_ln2_b': (0.0, 0.8),
     'L0_cond_ada_b': (0.0, 0.1),
     'L0_cond_qkv_b': (0.0, 0.637),
     'L0_cond_proj_b': (0.0, 0.285),
     'L0_cond_fc1_b': (0.0, 0.51),
     'L0_cond_fc2_b': (0.0, 0.329)}
    factors = {'L0_cond_qkv_w': 3.158, 'L0_cond_proj_w': 2.772}
    for name, (base, spread) in spreads.items():
        noise = np.random.default_rng([zlib.crc32(name.encode()), seed]).standard_normal(out[name].shape)
        drawn = base * np.exp(spread * noise) if base else spread * noise
        out[name] = jnp.asarray(drawn.astype(out[name].dtype))
    for name, factor in factors.items():
        out[name] = (out[name] * factor).astype(out[name].dtype)
    return out
```

```python
from contextlib import ExitStack

import numpy as np

import concourse.bass as bass
from concourse import mybir

F32 = mybir.dt.float32
F32R = mybir.dt.float32r
ALU = mybir.AluOpType
ACT = mybir.ActivationFunctionType
AX_X = mybir.AxisListType.X

P = 128
B, L, D = 2, 2048, 512
H, HD = 16, 32
FF = 4 * D
LN_EPS = 1e-5
KT = D // P
FT = FF // P
CH = 512
CPB = L // CH
TT = CH // P
HG = P // HD
NG = H // HG
NKT = L // P
SCALE = 1.0 / float(np.sqrt(np.float32(HD)))

R_LN1W, R_LN1B, R_LN2W, R_LN2B = 0, 4, 8, 12
R_ADAB = 16
R_QKB = 40
R_FC1B = 48
R_C = 64
N_ROWS = 72


def split_terms(a_hi, a_lo, b_hi, b_lo):
    return ((a_hi, b_hi), (a_hi, b_lo), (a_lo, b_hi))


def lower_half(nc, ctx, name, shape):
    with nc.sbuf_tensor(f"{name}_raw", shape, F32) as raw:
        pass
    return raw, ctx.enter_context(nc.sbuf_tensor(name, shape, F32R))


def build_qkv(nc, t, ins):
    NOUT = 2 * KT + TT
    NBANK = 6
    with ExitStack() as ctx:
        def sb(name, shape, dt=F32):
            return ctx.enter_context(nc.sbuf_tensor(name, shape, dt))

        def sem(name):
            return ctx.enter_context(nc.semaphore(name))

        rows = sb("rows", [N_ROWS, P])
        ada = sb("ada", [P, KT, 6 * D])
        expc = sb("expc", [P, B * KT])
        den = sb("den", [P, B * KT])
        rden = sb("rden", [P, B * KT])
        silu = sb("silu", [P, B, KT])
        silu_rep = sb("silu_rep", [P, B, KT, P])
        mod = sb("mod", [P, B, 16])
        tmp = sb("tmp", [P, 2, B, KT])
        adab = sb("adab", [P, 2, D])
        x_in = [sb(f"x_in{n}", [P, TT, D]) for n in range(2)]
        stats = sb("stats", [P, TT, 6])
        mv = sb("mv", [P, TT, 2])
        var_eps = sb("var_eps", [P, TT])
        rstd = sb("rstd", [P, TT])
        xn = [sb(f"xn{n}", [P, D]) for n in range(2)]
        h32 = [sb(f"h32_{n}", [P, KT, P]) for n in range(2)]
        hT_hi = [sb(f"hT_hi{n}", [P, KT, CH], F32R) for n in range(2)]
        hT_lo = [sb(f"hT_lo{n}", [P, KT, CH], F32R) for n in range(2)]
        qk_st = [sb(f"qk_st{n}", [P, 2, CH], F32R) for n in range(4)]
        v_st = [sb(f"v_st{n}", [P, TT, D]) for n in range(2)]
        tr_ps = [ctx.enter_context(nc.psum_tensor(f"tr_ps{n}", [P, KT, P], F32)) for n in range(2)]
        out_ps = [ctx.enter_context(nc.psum_tensor(f"out_ps{n}", [P, CH], F32)) for n in range(NBANK)]

        rows_loaded, bc_loaded, qkv_loaded = sem("rows_loaded"), sem("bc_loaded"), sem("qkv_loaded")
        ada_loaded = [sem(f"ada_loaded{n}") for n in range(2)]
        ident_zero, ident_done, consts_set = sem("ident_zero"), sem("ident_done"), sem("consts_set")
        rows_turned, cols_done, expc_done = sem("rows_turned"), sem("cols_done"), sem("expc_done")
        den_done, rden_done, silu_done, rep_done = sem("den_done"), sem("rden_done"), sem("silu_done"), sem("rep_done")
        mod_summed, mod_done, tmp_done, cols_mod = sem("mod_summed"), sem("mod_done"), sem("tmp_done"), sem("cols_mod")
        gates_done = sem("gates_done")
        w_hi_done, w_lo_done = sem("w_hi_done"), sem("w_lo_done")
        waits_passed = sem("waits_passed")
        x_loaded = [sem(f"x_loaded{n}") for n in range(2)]
        stats_done, mv_done, eps_done, rstd_done = sem("stats_done"), sem("mv_done"), sem("eps_done"), sem("rstd_done")
        xn_done, turned, h32_done, hT_hi_done, hT_done = sem("xn_done"), sem("turned"), sem("h32_done"), sem("hT_hi_done"), sem("hT_done")
        out_full, hi_done = sem("out_full"), sem("hi_done")
        out_free = sem("out_free")
        qk_stored = [sem(f"qk_stored{n}") for n in range(4)]
        v_stored = [sem(f"v_stored{n}") for n in range(2)]

        x_v = ins["x"].rearrange("b (t p) d -> b p t d", p=P)
        v_v = t.v_dram[:, :, :].rearrange("b (t p) d -> b p t d", p=P)
        block = ctx.enter_context(nc.Block())

        @block.sync
        def _(sp):
            def load_x(i, b, normalised=None):
                if normalised is not None:
                    sp.wait_ge(xn_done, normalised)
                    sp.sem_inc(waits_passed, 1)
                sp.dma_start(x_in[b][:, :, :], x_v[b, :, bass.ds(i * TT, TT), :]).then_inc(x_loaded[b], 16)

            def chunk(i, b, more):
                c = 2 * i + b
                if more:
                    load_x(i + 1, b, TT * c + TT)
                for m in range(2 * KT):
                    sp.wait_ge(out_free, NOUT * c + m + 1 + NBANK)
                    sp.sem_inc(waits_passed, 1)
                    sp.dma_start(t.qk_dram[m // KT, :, m % KT, :, b, bass.ds(i * CH, CH)].rearrange("s p t -> p s t"),
                                 qk_st[m % 4][:, :, :].bitcast(F32)).then_inc(qk_stored[m % 4], 16)
                sp.wait_ge(out_free, NOUT * c + NOUT + NBANK)
                sp.sem_inc(waits_passed, 1)
                sp.dma_start(v_v[b, :, bass.ds(i * TT, TT), :], v_st[b][:, :, :]).then_inc(v_stored[b], 16)

            for at, name in ((R_C, "cond"), (R_LN1W, "ln1_w"), (R_LN1B, "ln1_b"), (R_LN2W, "ln2_w"), (R_LN2B, "ln2_b"),
                             (R_ADAB, "ada_b"), (R_FC1B, "fc1_b"), (R_QKB, "qkv_b")):
                v = ins[name][0:2 * D] if name == "qkv_b" else ins[name]
                v = v.rearrange("b (r p) -> (b r) p", p=P) if name == "cond" else v.rearrange("(r p) -> r p", p=P)
                sp.dma_start(rows[at:at + v.shape[0], :], v).then_inc(rows_loaded, 16)
            ada_v = ins["ada_w"].rearrange("(k p) n -> p k n", p=P)
            sp.dma_start(ada[:, :, 0:2 * D], ada_v[:, :, 0:2 * D]).then_inc(ada_loaded[0], 16)
            load_x(0, 1)
            sp.dma_start(t.v_bias[:, :], ins["qkv_b"][None, 2 * D:3 * D].to_broadcast([P, D])).then_inc(bc_loaded, 16)
            for n, g in enumerate((2, 5)):
                sp.dma_start(adab[:, n, :], ins["ada_b"][None, g * D:(g + 1) * D].to_broadcast([P, D])).then_inc(bc_loaded, 16)
            sp.dma_start(ada[:, :, 2 * D:6 * D], ada_v[:, :, 2 * D:6 * D]).then_inc(ada_loaded[1], 16)
            with sp.Fori(0, CPB - 1) as i:
                chunk(i, 0, True)
                chunk(i, 1, True)
            chunk(CPB - 1, 0, False)
            chunk(CPB - 1, 1, False)
            for s in qk_stored:
                sp.wait_ge(s, 16 + 16 * 2 * B * CPB)
            for s in v_stored:
                sp.wait_ge(s, 16 + 16 * CPB)

        @block.gpsimd
        def _(pool):
            def rstds(c, k):
                pool.wait_ge(eps_done, TT * c + k + 1)
                nc.gpsimd.tensor_tensor(rstd[:, k:k + 1], var_eps[:, k:k + 1], t.minus_half[:, :], ALU.pow).then_inc(rstd_done, 1)

            nc.gpsimd.memset(t.ident[:, :], 0.0).then_inc(ident_zero, 1)
            nc.gpsimd.memset(t.minus_half[:, :], -0.5).then_inc(consts_set, 1)
            pool.wait_ge(ident_zero, 1)
            nc.gpsimd.affine_select(out=t.ident[:, :], in_=t.ident[:, :], compare_op=ALU.not_equal, fill=1.0, base=0,
                                    pattern=[[-1, P]], channel_multiplier=1).then_inc(ident_done, 1)
            nc.gpsimd.memset(t.ones[:, :], 1.0).then_inc(consts_set, 1)
            pool.wait_ge(consts_set, 2)
            with pool.Fori(0, B * CPB) as c:
                for k in range(TT):
                    rstds(c, k)

        @block.tensor
        def _(pe):
            def transposes(c, k, first=False):
                g = TT * c + k
                pe.wait_ge(xn_done, g + 1)
                if not first:
                    pe.wait_ge(h32_done, g - 1)
                for j in range(KT):
                    last = nc.tensor.transpose(tr_ps[k % 2][:, j, :], xn[k % 2][:, j * P:(j + 1) * P], t.ident[:, :])
                last.then_inc(turned, 1)

            def output(c, b, o):
                bank = out_ps[o % NBANK]
                pe.wait_ge(out_free, NOUT * c + o + 1)
                n = 0
                for k in range(KT):
                    h_hi, h_lo = hT_hi[b][:, k, :], hT_lo[b][:, k, :]
                    if o < 2 * KT:
                        cols = slice(o * P, (o + 1) * P)
                        pairs = split_terms(t.wqkv_hi[:, k, cols], t.wqkv_lo[:, k, cols], h_hi, h_lo)
                    else:
                        tok = slice((o - 2 * KT) * P, (o - 2 * KT + 1) * P)
                        pairs = split_terms(h_hi[:, tok], h_lo[:, tok], t.wqkv_hi[:, k, 2 * D:3 * D], t.wqkv_lo[:, k, 2 * D:3 * D])
                    for lhs, rhs in pairs:
                        last = nc.tensor.matmul(bank[:, :], lhs, rhs, start=(n == 0), stop=(n == 3 * KT - 1))
                        n += 1
                last.then_inc(out_full, 1)

            def columns(bank, n):
                for m in range(2 * KT):
                    at = 3 * n * D + m * P
                    for k in range(KT):
                        last = nc.tensor.matmul(bank[:, 2 * m:2 * m + 2], ada[:, k, at:at + P], silu[:, :, k],
                                                start=(k == 0), stop=(k == KT - 1))
                last.then_inc(mod_summed, 1)

            def gate(bank, n, b):
                at = (2, 5)[n] * D
                for k in range(KT):
                    last = nc.tensor.matmul(bank[:, :], silu_rep[:, b, k, :], ada[:, k, at:at + D],
                                            start=(k == 0), stop=(k == KT - 1))
                last.then_inc(out_full, 1)

            def chunk(i, b, more):
                c = 2 * i + b
                pe.wait_ge(hT_done, TT * c + TT)
                for k in range(TT):
                    output(c, b, 3 * k)
                    output(c, b, 3 * k + 1)
                    if more:
                        transposes(c + 1, k)
                    output(c, b, 3 * k + 2)

            pe.wait_ge(ident_done, 1)
            pe.wait_ge(rows_loaded, 16 * 8)
            nc.tensor.transpose(out_ps[0][:, 0:N_ROWS], rows[:, :], t.ident[0:N_ROWS, 0:N_ROWS]).then_inc(rows_turned, 1)
            transposes(0, 0, True)
            transposes(0, 1, True)
            pe.wait_ge(silu_done, 1)
            pe.wait_ge(ada_loaded[0], 16)
            columns(out_ps[1], 0)
            transposes(0, 2)
            transposes(0, 3)
            pe.wait_ge(w_lo_done, KT)
            with pe.Fori(0, CPB - 1) as i:
                chunk(i, 0, True)
                chunk(i, 1, True)
            chunk(CPB - 1, 0, True)
            chunk(CPB - 1, 1, False)
            pe.wait_ge(rep_done, B * KT)
            pe.wait_ge(ada_loaded[1], 16)
            for n in range(2 * B):
                pe.wait_ge(out_free, NOUT * B * CPB + n + 1)
                gate(out_ps[n % NBANK], n // B, n % B)
            pe.wait_ge(out_free, NOUT * B * CPB + 2 * B + 1)
            columns(out_ps[2 * B % NBANK], 1)

        @block.scalar
        def _(act):
            def modulate(c, b, k, first=False):
                g = TT * c + k
                act.wait_ge(turned, g + 1)
                if not first:
                    act.wait_ge(hT_done, g - 1)
                for j in range(KT):
                    last = nc.scalar.activation(h32[k % 2][:, j, :], tr_ps[k % 2][:, j, :], ACT.Identity,
                                                bias=t.mod_b[:, 0, b, j:j + 1], scale=t.mod_w[:, 0, b, j:j + 1])
                last.then_inc(h32_done, 1)

            def upper(c, b, o):
                act.wait_ge(out_full, NOUT * c + o + 1)
                act.wait_ge(qk_stored[o % 4], 16 * (2 * c + o // 4 + 1))
                nc.scalar.activation(qk_st[o % 4][:, 0, :], out_ps[o % NBANK][:, :], ACT.Identity,
                                     bias=t.cols[:, R_QKB + o:R_QKB + o + 1]).then_inc(hi_done, 1)

            def chunk(i, b, more):
                c = 2 * i + b
                for k in range(TT):
                    for o in (3 * k, 3 * k + 1):
                        if o < 2 * KT:
                            upper(c, b, o)
                    if more:
                        modulate(c + 1, 1 - b, k)
                    if 3 * k + 2 < 2 * KT:
                        upper(c, b, 3 * k + 2)

            x_view = x_v[0, :, 0:TT, :]
            act.dma_start(x_in[0][:, :, :], x_view).then_inc(x_loaded[0], 16)
            for k in range(KT):
                act.dma_start(t.wqkv_raw[:, k, :], ins["qkv_w"][k * P:(k + 1) * P, :]).then_inc(qkv_loaded, 16)
            act.wait_ge(cols_done, 1)
            nc.scalar.activation(expc[:, :], t.cols[:, R_C:R_C + B * KT], ACT.Exp, scale=-1.0).then_inc(expc_done, 1)
            act.wait_ge(qkv_loaded, 16 * KT)
            for k in range(KT):
                nc.scalar.activation(t.wqkv_hi[:, k, :], t.wqkv_raw[:, k, :], ACT.Copy).then_inc(w_hi_done, 1)
            act.wait_ge(cols_mod, 4)
            for k in range(TT):
                modulate(0, 0, k, k < 2)
            with act.Fori(0, CPB - 1) as i:
                chunk(i, 0, True)
                chunk(i, 1, True)
            chunk(CPB - 1, 0, True)
            chunk(CPB - 1, 1, False)

        @block.vector
        def _(dve):
            def tile_stats(i, b, k):
                g = TT * (2 * i + b) + k
                dve.wait_ge(x_loaded[b], 16 * i + 16)
                nc.vector.bn_stats(stats[:, k, :], x_in[b][:, k, :]).then_inc(stats_done, 1)
                dve.wait_ge(stats_done, g + 1)
                nc.vector.tensor_copy(t.scrap[:, 8:10], t.cols[:, 0:2])
                nc.vector.bn_aggr(mv[:, k, :], stats[:, k, :]).then_inc(mv_done, 1)
                dve.wait_ge(mv_done, g + 1)
                nc.vector.tensor_scalar(var_eps[:, k:k + 1], mv[:, k, 1:2], LN_EPS, None, ALU.add).then_inc(eps_done, 1)

            def normalise(i, b, k, first=False):
                g = TT * (2 * i + b) + k
                dve.wait_ge(rstd_done, g + 1)
                if not first:
                    dve.wait_ge(turned, g - 1)
                nc.vector.tensor_scalar(xn[k % 2][:, :], x_in[b][:, k, :], mv[:, k, 0:1], rstd[:, k:k + 1],
                                        ALU.subtract, ALU.mult).then_inc(xn_done, 1)

            def split_h(i, b, k):
                g = TT * (2 * i + b) + k
                tok = slice(k * P, (k + 1) * P)
                dve.wait_ge(h32_done, g + 1)
                nc.vector.tensor_copy(hT_hi[b][:, :, tok], h32[k % 2][:, :, :]).then_inc(hT_hi_done, 1)
                dve.wait_ge(hT_hi_done, g + 1)
                nc.vector.tensor_tensor(hT_lo[b][:, :, tok], h32[k % 2][:, :, :], hT_hi[b][:, :, tok].bitcast(F32),
                                        ALU.subtract).then_inc(hT_done, 1)

            def evacuate(i, b, o):
                c = 2 * i + b
                bank = out_ps[o % NBANK]
                if o < 2 * KT:
                    dve.wait_ge(hi_done, 2 * KT * c + o + 1)
                    nc.vector.scalar_tensor_tensor(qk_st[o % 4][:, 1, :], bank[:, :], t.cols[:, R_QKB + o:R_QKB + o + 1],
                                                   qk_st[o % 4][:, 0, :].bitcast(F32), ALU.add, ALU.subtract).then_inc(out_free, 1)
                else:
                    dve.wait_ge(out_full, NOUT * c + o + 1)
                    if o == 2 * KT:
                        dve.wait_ge(v_stored[b], 16 * i + 16)
                    nc.vector.tensor_tensor(v_st[b][:, o - 2 * KT, :], bank[:, :], t.v_bias[:, :], ALU.add).then_inc(out_free, 1)

            def chunk(i, b, more):
                ni, nb = (i, 1) if b == 0 else (i + 1, 0)
                for k in range(TT):
                    if more:
                        tile_stats(ni, nb, k)
                    evacuate(i, b, 3 * k)
                    if more:
                        normalise(ni, nb, k)
                    evacuate(i, b, 3 * k + 1)
                    if more:
                        split_h(ni, nb, k)
                    evacuate(i, b, 3 * k + 2)

            def modulation(bank, n):
                dve.wait_ge(mod_summed, n + 1)
                for b in range(B):
                    nc.vector.tensor_tensor(mod[:, b, 8 * n:8 * n + 8], bank[:, 0:4 * KT].rearrange("p (m b) -> p m b", b=B)[:, :, b],
                                            t.cols[:, R_ADAB + 12 * n:R_ADAB + 12 * n + 8], ALU.add).then_inc(mod_done, 1)
                dve.wait_ge(mod_done, 2 * n + 2)
                lw, lb = ((R_LN1W, R_LN1B), (R_LN2W, R_LN2B))[n]
                for b in range(B):
                    scale = mod[:, b, 8 * n + 4:8 * n + 8]
                    nc.vector.scalar_tensor_tensor(t.mod_w[:, n, b, :], scale, 1.0, t.cols[:, lw:lw + 4], ALU.add, ALU.mult).then_inc(cols_mod, 1)
                    nc.vector.scalar_tensor_tensor(tmp[:, n, b, :], scale, 1.0, t.cols[:, lb:lb + 4], ALU.add, ALU.mult).then_inc(tmp_done, 1)
                dve.wait_ge(tmp_done, 2 * n + 2)
                for b in range(B):
                    nc.vector.tensor_tensor(t.mod_b[:, n, b, :], tmp[:, n, b, :], mod[:, b, 8 * n:8 * n + 4], ALU.add).then_inc(cols_mod, 1)

            dve.wait_ge(rows_turned, 1)
            nc.vector.tensor_copy(t.cols[:, :], out_ps[0][:, 0:N_ROWS]).then_inc(cols_done, 1)
            dve.wait_ge(expc_done, 1)
            nc.vector.tensor_scalar(den[:, :], expc[:, :], 1.0, None, ALU.add).then_inc(den_done, 1)
            dve.wait_ge(den_done, 1)
            nc.vector.reciprocal(rden[:, :], den[:, :]).then_inc(rden_done, 1)
            dve.wait_ge(rden_done, 1)
            dve.wait_ge(cols_done, 1)
            nc.vector.tensor_tensor(silu[:, :, :], t.cols[:, R_C:R_C + B * KT].rearrange("p (b k) -> p b k", b=B),
                                    rden[:, :].rearrange("p (b k) -> p b k", b=B), ALU.mult).then_inc(silu_done, 1)
            for k in range(TT):
                tile_stats(0, 0, k)
            normalise(0, 0, 0, True)
            normalise(0, 0, 1, True)
            for k in range(KT):
                dve.wait_ge(w_hi_done, k + 1)
                nc.vector.tensor_tensor(t.wqkv_lo[:, k, :], t.wqkv_raw[:, k, :], t.wqkv_hi[:, k, :].bitcast(F32),
                                        ALU.subtract).then_inc(w_lo_done, 1)
            modulation(out_ps[1], 0)
            nc.vector.memset(t.scrap[:, 0:1], 0.0).then_inc(out_free, NBANK)
            for n, stored in enumerate(qk_stored + v_stored):
                nc.vector.memset(t.scrap[:, n + 1:n + 2], 0.0).then_inc(stored, 16)
            for k in range(TT):
                if k >= 2:
                    normalise(0, 0, k)
                split_h(0, 0, k)
            dve.wait_ge(silu_done, 1)
            for b in range(B):
                for k in range(KT):
                    nc.vector.tensor_copy(silu_rep[:, b, k, :], silu[:, b, k:k + 1].to_broadcast([P, P])).then_inc(rep_done, 1)
            dve.wait_ge(bc_loaded, 48)
            with dve.Fori(0, CPB - 1) as i:
                chunk(i, 0, True)
                chunk(i, 1, True)
            chunk(CPB - 1, 0, True)
            chunk(CPB - 1, 1, False)
            for n in range(2 * B):
                dve.wait_ge(out_full, NOUT * B * CPB + n + 1)
                nc.vector.tensor_tensor(t.gates[:, n // B, n % B, :], out_ps[n % NBANK][:, :], adab[:, n // B, :], ALU.add).then_inc(gates_done, 1)
            modulation(out_ps[2 * B % NBANK], 1)
            dve.wait_ge(gates_done, 2 * B)
            dve.wait_ge(cols_mod, 8)


def build_attention(nc, t):
    STEPS = 2 * CPB
    MX = HG * TT * 2
    RING = 4
    AHEAD = 4
    LAG = 2
    TURN_AT = (MX - AHEAD) // 2
    PAIRS, QUADS = NKT // 2, NKT // 4
    BY_DVE, BY_POOL = (0, 2), (1,)
    QUAD_AT = {4 * g + 5 + d: [(g, j) for j in js] for g in BY_DVE for d, js in ((0, (0,)), (1, (1,)), (2, (2, 3)))}
    with ExitStack() as ctx:
        def sb(name, shape, dt=F32):
            return ctx.enter_context(nc.sbuf_tensor(name, shape, dt))

        def sem(name):
            return ctx.enter_context(nc.semaphore(name))

        ks = [sb(f"ks{n}", [3 * HD + 1, HG, L], F32R) for n in range(2)]
        qs = [sb(f"qs{n}", [3 * HD + 1, HG, CH], F32R) for n in range(CPB)]
        vs = [sb(f"vs{n}", [P, NKT, P]) for n in range(2)]
        prob = [sb(f"prob{n}", [P, HG, CH]) for n in range(RING)]
        pair = [sb(f"pair{n}", [P, HG, CH]) for n in range(4)]
        mpart = sb("mpart", [P, HG * TT, 2])
        m16 = sb("m16", [P, HG * TT])
        mrow = sb("mrow", [HG * TT, P], F32R)
        o_sb = sb("o_sb", [P, CH])
        den_sb = sb("den_sb", [P, CH])
        rec = sb("rec", [P, CH])
        aT = [sb(f"aT{n}", [P, CH]) for n in range(2)]

        mx_ps = [ctx.enter_context(nc.psum_tensor(f"mx_ps{n}", [P, 2, CH], F32)) for n in range(2)]
        s_ps = [ctx.enter_context(nc.psum_tensor(f"s_ps{n}", [P, CH], F32)) for n in range(2)]
        o_ps = ctx.enter_context(nc.psum_tensor("o_ps", [P, CH], F32))
        den_ps = ctx.enter_context(nc.psum_tensor("den_ps", [P, CH], F32))

        waits_passed = sem("waits_passed")
        k_loaded = [sem(f"k_loaded{n}") for n in range(2)]
        v_loaded = [sem(f"v_loaded{n}") for n in range(2)]
        q_loaded = [sem(f"q_loaded{n}") for n in range(CPB)]
        m_loaded = [sem(f"m_loaded{n}") for n in range(CPB)]
        ones_set = sem("ones_set")
        mx_full = sem("mx_full")
        mx_free = sem("mx_free")
        m16_done, m_turned, mrow_done = sem("m16_done"), sem("m_turned"), sem("mrow_done")
        s_full = sem("s_full")
        exp_done = sem("exp_done")
        prob_free = sem("prob_free")
        pair_done = sem("pair_done")
        quad_done, pool_quad_done = sem("quad_done"), sem("pool_quad_done")
        quad_free = sem("quad_free")
        o_copied = sem("o_copied")
        den_copied = sem("den_copied")
        rec_done, norm_done = sem("rec_done"), sem("norm_done")
        a_stored = [sem(f"a_stored{n}") for n in range(2)]

        block = ctx.enter_context(nc.Block())
        v_v = t.v_dram[:, :, :].rearrange("b (t p) d -> b p t d", p=P)

        def after(i, b, c, n=1):
            s = 4 * b + c + n
            return (i if s < STEPS else i + 1), (s // CPB) % 2, s % CPB

        @block.sync
        def _(sp):
            def load_kv(i, b, free=None):
                if free is not None:
                    sp.wait_ge(quad_free, free)
                    sp.sem_inc(waits_passed, 1)
                src = t.qk_dram[1, :, bass.ds(i, 1), :, b, :].rearrange("s o (j p) t -> (s o) p j t", p=HD)
                for at, half in enumerate((0, 0, 1)):
                    sp.dma_start(ks[b][at * HD:(at + 1) * HD, :, :].bitcast(F32), src[half]).then_inc(k_loaded[b], 16)
                sp.dma_start(vs[b][:, :, :], v_v[b, :, :, bass.ds(i * P, P)]).then_inc(v_loaded[b], 16)

            def load_q(i, b, c, used=None):
                if used is not None:
                    sp.wait_ge(s_full, used)
                    sp.sem_inc(waits_passed, 1)
                src = t.qk_dram[0, :, bass.ds(i, 1), :, b, c * CH:(c + 1) * CH].rearrange("s o (j p) t -> (s o) p j t", p=HD)
                for at, half in enumerate((0, 1, 0)):
                    sp.dma_start(qs[c][at * HD:(at + 1) * HD, :, :].bitcast(F32), src[half]).then_inc(q_loaded[c], 16)

            def store_max(s, c):
                sp.wait_ge(mrow_done, s + 1)
                sp.dma_start(qs[c][3 * HD:3 * HD + 1, :, :].bitcast(F32).rearrange("o j (q p) -> o (j q) p", p=P),
                             mrow[:, :].bitcast(F32)).then_inc(m_loaded[c], 16)

            def store_a(i, b, c, s):
                sp.wait_ge(norm_done, s + 2)
                sp.sem_inc(waits_passed, 1)
                sp.dma_start(t.a_dram[bass.ds(i, 1), :, b, c * CH:(c + 1) * CH].rearrange("o p t -> (o p) t"),
                             aT[c % 2][:, :]).then_inc(a_stored[c % 2], 16)

            def step(i, b, c, final, first):
                s = STEPS * i + 4 * b + c
                if not (final and 4 * b + c + 3 >= STEPS):
                    load_q(*after(i, b, c, 3), used=None if first else HG * NKT * s)
                if c == 0 and not (final and b == 1):
                    load_kv(*after(i, b, 0, CPB)[:2], free=None if first else QUADS * s + 2)
                if not first:
                    pi, pb, pc = (i, b, c - 1) if c else (i, 0, CPB - 1) if b else (i - 1, 1, CPB - 1)
                    store_a(pi, pb, pc, s - 1)
                if not (final and 4 * b + c == STEPS - 1):
                    store_max(s + 1, (c + 1) % CPB)

            load_q(0, 0, 0)
            load_kv(0, 0)
            load_q(0, 0, 1)
            load_q(0, 0, 2)
            store_max(0, 0)
            for n in range(STEPS):
                step(0, n // CPB, n % CPB, False, n == 0)
            with sp.Fori(1, NG - 1) as i:
                for n in range(STEPS):
                    step(i, n // CPB, n % CPB, False, False)
            for n in range(STEPS):
                step(NG - 1, n // CPB, n % CPB, True, False)
            store_a(NG - 1, 1, CPB - 1, NG * STEPS - 1)
            for s in a_stored:
                sp.wait_ge(s, 16 * NG * STEPS // 2)

        @block.gpsimd
        def _(pool):
            with pool.Fori(0, NG) as i:
                for n in range(STEPS):
                    s = STEPS * i + n
                    for p in range(PAIRS):
                        if p % 2 == 0:
                            pool.wait_ge(quad_free, QUADS * s + p // 2 + 1)
                        for j in range(HG):
                            pool.wait_ge(exp_done, HG * (NKT * s + 2 * p + 1) + j + 1 + 2)
                            nc.gpsimd.tensor_tensor(pair[p % 4][:, j, :], prob[2 * p % RING][:, j, :],
                                                    prob[(2 * p + 1) % RING][:, j, :], ALU.add).then_inc(pair_done, 1)
                        if p % 2 == 1 and p // 2 in BY_POOL:
                            even, odd = pair[(p - 1) % 4], pair[p % 4]
                            for j in range(HG):
                                pool.wait_ge(pair_done, HG * (PAIRS * s + p) + j + 1)
                                nc.gpsimd.tensor_tensor(even[:, j, :], even[:, j, :], odd[:, j, :], ALU.add).then_inc(pool_quad_done, 1)

        @block.tensor
        def _(pe):
            def max_slot(s, b, c, k):
                j, q, half = k // (2 * TT), k // 2 % TT, k % 2
                if k == 1:
                    pe.wait_ge(mrow_done, s)
                pe.wait_ge(mx_free, MX * s + k + 1)
                for e in range(2):
                    at = (2 * half + e) * CH
                    last = nc.tensor.matmul(mx_ps[k % 2][:, e, :], qs[c][0:3 * HD, j, q * P:(q + 1) * P],
                                            ks[b][0:3 * HD, j, at:at + CH], start=True, stop=True)
                last.then_inc(mx_full, 1)

            def turn_max(s):
                pe.wait_ge(m16_done, s + 1)
                nc.tensor.transpose(mx_ps[1][0:HG * TT, 0, 0:P], m16[:, :], t.ident[:, :]).then_inc(m_turned, 1)

            def max_begin(i, b, c, k):
                s = STEPS * i + 4 * b + c
                if k == 0:
                    pe.wait_ge(q_loaded[c], 48 * (2 * i + b) + 48)
                if k == 0 and c == 0:
                    pe.wait_ge(k_loaded[b], 48 * i + 48)
                max_slot(s, b, c, k)

            def score(s, b, c, kt, j):
                pe.wait_ge(exp_done, HG * (NKT * s + kt) + j + 1)
                nc.tensor.matmul(s_ps[j % 2][:, :], ks[b][:, j, kt * P:(kt + 1) * P], qs[c][:, j, :],
                                 start=True, stop=True).then_inc(s_full, 1)

            def values(s, b, kt):
                if kt == 0:
                    pe.wait_ge(o_copied, s + 1)
                pe.wait_ge(exp_done, HG * (NKT * s + kt + 1) + 2)
                for j in range(HG):
                    last = nc.tensor.matmul(o_ps[j * HD:(j + 1) * HD, :], vs[b][:, kt, j * HD:(j + 1) * HD],
                                            prob[kt % RING][:, j, :], start=(kt == 0), stop=(kt == NKT - 1))
                last.then_inc(prob_free, 1)

            def key_sums(s, p):
                g = p // 2
                if g in BY_DVE:
                    pe.wait_ge(quad_done, HG * (len(BY_DVE) * s + BY_DVE.index(g) + 1))
                elif g in BY_POOL:
                    pe.wait_ge(pool_quad_done, HG * (len(BY_POOL) * s + BY_POOL.index(g) + 1))
                else:
                    pe.wait_ge(pair_done, HG * (PAIRS * s + p + 1))
                if p == 0:
                    pe.wait_ge(den_copied, s + 1)
                for j in range(HG):
                    last = nc.tensor.matmul(den_ps[j * HD:(j + 1) * HD, :], t.ones[:, 0:HD], pair[p % 4][:, j, :],
                                            start=(p == 0), stop=(p == PAIRS - 1))
                if g < QUADS - 1 or p % 2 == 1:
                    last.then_inc(quad_free, 1)

            def step(i, b, c, final, first):
                n = 4 * b + c
                s = STEPS * i + n
                ni, nb, ncx = after(i, b, c)
                with_max = not (final and n == STEPS - 1)
                begin_max = not (final and n >= STEPS - 2)
                pe.wait_ge(m_loaded[c], 16 * (2 * i + b) + 16)
                if c == 0:
                    pe.wait_ge(v_loaded[b], 16 * i + 16)
                for kt in range(NKT):
                    score(s, b, c, kt, 0)
                    if kt >= LAG:
                        values(s, b, kt - LAG)
                    elif not first:
                        values(s - 1, (n - 1) // CPB % 2, NKT - LAG + kt)
                    score(s, b, c, kt, 1)
                    score(s, b, c, kt, 2)
                    if with_max and kt < TURN_AT:
                        max_slot(s + 1, nb, ncx, AHEAD + 2 * kt)
                        max_slot(s + 1, nb, ncx, AHEAD + 2 * kt + 1)
                    if begin_max and kt == TURN_AT:
                        max_begin(*after(i, b, c, 2), 0)
                    if with_max and kt == TURN_AT:
                        turn_max(s + 1)
                    if begin_max and kt == TURN_AT + 1:
                        max_begin(*after(i, b, c, 2), 2)
                        max_begin(*after(i, b, c, 2), 3)
                    score(s, b, c, kt, 3)
                    if kt in (8, 12):
                        key_sums(s, kt // 2 - 4)
                    if kt < 3 and not first:
                        key_sums(s - 1, (4, 6, 7)[kt])
                    if begin_max and kt == TURN_AT:
                        max_begin(*after(i, b, c, 2), 1)

            pe.wait_ge(ones_set, 2)
            max_begin(0, 0, 0, 0)
            for k in range(1, MX):
                max_slot(0, 0, 0, k)
            turn_max(0)
            for k in range(AHEAD):
                max_begin(0, 0, 1, k)
            for n in range(STEPS):
                step(0, n // CPB, n % CPB, False, n == 0)
            with pe.Fori(1, NG - 1) as i:
                for n in range(STEPS):
                    step(i, n // CPB, n % CPB, False, False)
            for n in range(STEPS):
                step(NG - 1, n // CPB, n % CPB, True, False)
            s = NG * STEPS - 1
            for kt in range(NKT - LAG, NKT):
                values(s, 1, kt)
            for p in (4, 6, 7):
                key_sums(s, p)

        @block.scalar
        def _(act):
            def exponential(s, kt, j, first):
                act.wait_ge(s_full, HG * (NKT * s + kt) + j + 1)
                act.wait_ge(prob_free, NKT * s + kt + 1)
                if kt >= RING or not first:
                    act.wait_ge(pair_done, HG * (PAIRS * s + (kt - RING) // 2) + j + 1)
                nc.scalar.activation(prob[kt % RING][:, j, :], s_ps[j % 2][:, :], ACT.Exp, scale=SCALE).then_inc(exp_done, 1)

            def copy_outputs(s):
                act.wait_ge(prob_free, NKT * (s + 1) + RING)
                act.wait_ge(norm_done, s + 1)
                nc.scalar.activation(o_sb[:, :], o_ps[:, :], ACT.Copy).then_inc(o_copied, 1)

            def copy_denominators(s):
                act.wait_ge(quad_free, QUADS * (s + 1) + 2)
                act.wait_ge(norm_done, s + 1)
                nc.scalar.activation(den_sb[:, :], den_ps[:, :], ACT.Copy).then_inc(den_copied, 1)

            def step(i, n, first):
                s = STEPS * i + n
                for kt in range(NKT):
                    for j in range(HG):
                        exponential(s, kt, j, first)
                        if kt == LAG - 1 and j == 1 and not first:
                            copy_outputs(s - 1)
                        if kt == 3 and j == 1 and not first:
                            copy_denominators(s - 1)

            for n in range(STEPS):
                step(0, n, n == 0)
            with act.Fori(1, NG) as i:
                for n in range(STEPS):
                    step(i, n, False)
            copy_outputs(NG * STEPS - 1)
            copy_denominators(NG * STEPS - 1)

        @block.vector
        def _(dve):
            def maxima(s, k):
                dve.wait_ge(mx_full, MX * s + k + 1)
                nc.vector.tensor_reduce(mpart[:, k // 2, k % 2:k % 2 + 1], mx_ps[k % 2][:, :, :].rearrange("p e t -> p (e t)"),
                                        AX_X, ALU.max).then_inc(mx_free, 1)

            def combine(s):
                dve.wait_ge(mx_free, MX * (s + 1) + 2)
                nc.vector.tensor_reduce(m16[:, :], mpart[:, :, :], AX_X, ALU.max).then_inc(m16_done, 1)

            def negate(s):
                dve.wait_ge(m_turned, s + 1)
                nc.vector.tensor_scalar(mrow[:, :], mx_ps[1][0:HG * TT, 0, 0:P], -1.0, None, ALU.mult).then_inc(mrow_done, 1)

            def add_pairs(s, g, j):
                dve.wait_ge(pair_done, HG * (PAIRS * s + 2 * g + 1) + j + 1)
                even, odd = pair[2 * g % 4], pair[(2 * g + 1) % 4]
                nc.vector.tensor_tensor(even[:, j, :], even[:, j, :], odd[:, j, :], ALU.add).then_inc(quad_done, 1)

            def reciprocals(s, quarter):
                at = slice(quarter * P, (quarter + 1) * P)
                nc.vector.reciprocal(rec[:, at], den_sb[:, at]).then_inc(rec_done, 1)

            def normalise(s, c, stored):
                dve.wait_ge(rec_done, 4 * (s + 1))
                dve.wait_ge(o_copied, s + 2)
                dve.wait_ge(a_stored[c % 2], stored)
                nc.vector.tensor_tensor(aT[c % 2][:, :], o_sb[:, :], rec[:, :], ALU.mult).then_inc(norm_done, 1)

            def step(i, b, c, final, first):
                n = 4 * b + c
                s = STEPS * i + n
                with_max = not (final and n == STEPS - 1)
                begin_max = not (final and n >= STEPS - 2)
                for kt in range(NKT):
                    if with_max and kt < TURN_AT:
                        maxima(s + 1, AHEAD + 2 * kt)
                        maxima(s + 1, AHEAD + 2 * kt + 1)
                    if with_max and kt == TURN_AT:
                        combine(s + 1)
                        dve.wait_ge(m_loaded[c], 16 * (2 * i + b) + 16)
                        negate(s + 1)
                    if begin_max and kt >= TURN_AT:
                        maxima(s + 2, 2 * (kt - TURN_AT))
                        maxima(s + 2, 2 * (kt - TURN_AT) + 1)
                    for g, j in QUAD_AT.get(kt, ()):
                        add_pairs(s, g, j)
                    if not first:
                        if kt == 4:
                            dve.wait_ge(den_copied, s + 1)
                            reciprocals(s - 1, 0)
                        if kt == 8:
                            reciprocals(s - 1, 1)
                            reciprocals(s - 1, 2)
                        if kt == 12:
                            reciprocals(s - 1, 3)
                            normalise(s - 1, (c - 1) % CPB, 16 * (4 * i + (n - 1) // 2) if n else 16 * (4 * i - 1))

            for free, (sem_, n) in enumerate(((mx_free, 2), (exp_done, 2), (prob_free, RING), (quad_free, 2), (o_copied, 1), (den_copied, 1), (norm_done, 1))):
                nc.vector.memset(t.scrap[:, free:free + 1], 0.0).then_inc(sem_, n)
            for b in range(2):
                nc.vector.memset(ks[b][3 * HD:3 * HD + 1, :, :].bitcast(F32), 1.0).then_inc(ones_set, 1)
            for k in range(MX):
                maxima(0, k)
            combine(0)
            negate(0)
            for k in range(AHEAD):
                maxima(1, k)
            for n in range(STEPS):
                step(0, n // CPB, n % CPB, False, n == 0)
            with dve.Fori(1, NG - 1) as i:
                for n in range(STEPS):
                    step(i, n // CPB, n % CPB, False, False)
            for n in range(STEPS):
                step(NG - 1, n // CPB, n % CPB, True, False)
            s = NG * STEPS - 1
            dve.wait_ge(den_copied, s + 2)
            for q in range(4):
                reciprocals(s, q)
            normalise(s, CPB - 1, 16 * (s // 2))


def build_mlp(nc, t, ins, out):
    GR = 2
    with ExitStack() as ctx:
        def sb(name, shape, dt=F32):
            return ctx.enter_context(nc.sbuf_tensor(name, shape, dt))

        def sem(name):
            return ctx.enter_context(nc.semaphore(name))

        wp_hi, w1_hi, w2_hi = sb("wp_hi", [P, KT, D], F32R), sb("w1_hi", [P, KT, FF], F32R), sb("w2_hi", [P, FT, D], F32R)
        wp_raw, wp_lo = lower_half(nc, ctx, "wp_lo", [P, KT, D])
        w1_raw, w1_lo = lower_half(nc, ctx, "w1_lo", [P, KT, FF])
        w2_raw, w2_lo = lower_half(nc, ctx, "w2_lo", [P, FT, D])
        bias_rows = sb("bias_rows", [HD + 1, 2, D], F32R)
        ones_rows = sb("ones_rows", [HD + 1, P], F32R)
        hT_hi = [sb(f"h2_hi{n}", [P, KT, CH], F32R) for n in range(2)]
        hT_lo = [sb(f"h2_lo{n}", [P, KT, CH], F32R) for n in range(2)]
        a32 = [sb(f"a32_{n}", [P, KT, P]) for n in range(2)]
        a_hi = sb("a_hi", [P, KT, P], F32R)
        a_lo = sb("a_lo", [P, KT, P], F32R)
        xt = [sb(f"xt{n}", [P, D]) for n in range(2)]
        stats = sb("stats2", [P, 6])
        mv = sb("mv2", [P, 2])
        var_eps = sb("var_eps2", [P, 1])
        rstd = sb("rstd2", [P, 1])
        proj = sb("proj", [P, D])
        xn = proj
        h32 = sb("h32m", [P, KT, P])
        g32 = [sb(f"g32_{n}", [P, CH]) for n in range(2)]
        brow = [g[0:1, :] for g in g32]
        g_hi = [sb(f"g_hi{n}", [P, CH], F32R) for n in range(GR)]
        g_lo = [sb(f"g_lo{n}", [P, CH], F32R) for n in range(GR)]
        res = [sb(f"res{n}", [P, D]) for n in range(2)]
        acc_ps = [ctx.enter_context(nc.psum_tensor(f"acc_ps{n}", [P, D], F32)) for n in range(TT)]
        f_ps = [ctx.enter_context(nc.psum_tensor(f"f_ps{n}", [P, CH], F32)) for n in range(2)]
        proj_ps = ctx.enter_context(nc.psum_tensor("proj_ps", [P, D], F32))
        tr_ps = ctx.enter_context(nc.psum_tensor("tr2_ps", [P, KT, P], F32))

        FC1_DONE, FC2_DONE = 1 + KT, 1 + 2 * KT
        fc2_v = ins["fc2_w"].rearrange("(k p) n -> p k n", p=P)
        pieces = [(ins["proj_w"].rearrange("(k p) n -> p k n", p=P), wp_raw[:, :, :], wp_hi[:, :, :], wp_lo[:, :, :])]
        pieces += [(ins["fc1_w"][k * P:(k + 1) * P, :], w1_raw[:, k, :], w1_hi[:, k, :], w1_lo[:, k, :]) for k in range(KT)]
        pieces += [(fc2_v[:, k:k + KT, :], w2_raw[:, k:k + KT, :], w2_hi[:, k:k + KT, :],
                    w2_lo[:, k:k + KT, :]) for k in range(0, FT, KT)]

        w_loaded = [sem(f"w_loaded{n}") for n in range(len(pieces))]
        w_hi_done, w_lo_done = sem("w2_hi_done"), sem("w2_lo_done")
        brow_loaded, rows_set, brow_hi, brow_lo = sem("brow_loaded"), sem("rows_set"), sem("brow_hi"), sem("brow_lo")
        waits_passed = sem("waits_passed")
        a_loaded = [sem(f"a_loaded{n}") for n in range(2)]
        x_loaded = [sem(f"xt_loaded{n}") for n in range(2)]
        a_hi_done, a_lo_done, proj_full, gated = sem("a_hi_done"), sem("a_lo_done"), sem("proj_full"), sem("gated")
        x1_done, stats_done, mv_done, eps_done, rstd_done = (sem("x1_done"), sem("stats2_done"), sem("mv2_done"),
                                                             sem("eps2_done"), sem("rstd2_done"))
        x1_stored = [sem(f"x1_stored{n}") for n in range(2)]
        xn_done, turned, h32_done, hT_hi_done, hT_done = (sem("xn2_done"), sem("turned2"), sem("h32m_done"),
                                                          sem("h2_hi_done"), sem("h2_done"))
        f_full = sem("f_full")
        f_free = sem("f_free")
        g_hi_done = sem("g_hi_done")
        g_done = sem("g_done")
        g_free = sem("g_free")
        acc_full = sem("acc_full")
        acc_free = sem("acc_free")
        acc_scaled = sem("acc_scaled")
        res_loaded = [sem(f"res_loaded{n}") for n in range(2)]
        out_stored = [sem(f"out_stored{n}") for n in range(2)]

        x_v = ins["x"].rearrange("b (t p) d -> b t p d", p=P)
        x1_v = t.x1_dram[:, :, :].rearrange("b (t p) d -> b t p d", p=P)
        out_v = out.rearrange("b (t p) d -> b t p d", p=P)
        block = ctx.enter_context(nc.Block())

        def nxt(i, b):
            return (i, 1) if b == 0 else (i + 1, 0)

        def prv(i, b):
            return (i, 0) if b == 1 else (i - 1, 1)

        def turns(eng, chunk):
            chunk(0, 0, True, True)
            chunk(0, 1, True, False)
            with eng.Fori(1, CPB - 1) as i:
                chunk(i, 0, True, False)
                chunk(i, 1, True, False)
            chunk(CPB - 1, 0, True, False)
            chunk(CPB - 1, 1, False, False)

        @block.sync
        def _(sp):
            def load_tile(i, b, k, first=False):
                c = 2 * i + b
                if not first:
                    sp.wait_ge(a_lo_done, TT * c + k - 1)
                    sp.sem_inc(waits_passed, 1)
                    sp.wait_ge(x1_stored[k % 2], 16 * (2 * c + k // 2))
                    sp.sem_inc(waits_passed, 1)
                    sp.wait_ge(xn_done, TT * c + k - 1)
                    sp.sem_inc(waits_passed, 1)
                sp.dma_start(a32[k % 2][:, :, :], t.a_dram[:, :, b, bass.ds(i * CH + k * P, P)].rearrange("g p t -> p g t")
                             ).then_inc(a_loaded[k % 2], 16)
                sp.dma_start(xt[k % 2][:, :], x_v[b, bass.ds(i * TT + k, 1), :, :].rearrange("o p d -> (o p) d")
                             ).then_inc(x_loaded[k % 2], 16)

            def store_x1(i, b, k):
                sp.wait_ge(x1_done, TT * (2 * i + b) + k + 1)
                sp.sem_inc(waits_passed, 1)
                sp.dma_start(x1_v[b, bass.ds(i * TT + k, 1), :, :].rearrange("o p d -> (o p) d"), xt[k % 2][:, :]
                             ).then_inc(x1_stored[k % 2], 16)

            def load_res(i, b, k, first=False):
                n = 2 * (2 * i + b) + k // 2
                if not first:
                    sp.wait_ge(out_stored[k % 2], 16 * n)
                    sp.sem_inc(waits_passed, 1)
                sp.wait_ge(x1_stored[k % 2], 16 * n + 16)
                sp.sem_inc(waits_passed, 1)
                sp.dma_start(res[k % 2][:, :], x1_v[b, bass.ds(i * TT + k, 1), :, :].rearrange("o p d -> (o p) d")
                             ).then_inc(res_loaded[k % 2], 16)

            def store_out(i, b, k):
                sp.wait_ge(acc_free, TT * (2 * i + b) + k + 1 + TT)
                sp.sem_inc(waits_passed, 1)
                sp.dma_start(out_v[b, bass.ds(i * TT + k, 1), :, :].rearrange("o p d -> (o p) d"), res[k % 2][:, :]
                             ).then_inc(out_stored[k % 2], 16)

            def results(i, b):
                store_out(i, b, 0)
                load_res(i, b, 2)
                store_out(i, b, 1)
                load_res(i, b, 3)
                store_out(i, b, 2)
                store_out(i, b, 3)

            def chunk(i, b, more, first):
                ni, nb = nxt(i, b)
                if more:
                    load_tile(ni, nb, 0)
                    load_tile(ni, nb, 1)
                if not first:
                    results(*prv(i, b))
                load_res(i, b, 0, first)
                load_res(i, b, 1, first)
                if more:
                    for k in range(TT):
                        store_x1(ni, nb, k)
                        if k + 2 < TT:
                            load_tile(ni, nb, k + 2)

            load_tile(0, 0, 0, True)
            load_tile(0, 0, 1, True)
            for n, name in enumerate(("proj_b", "fc2_b")):
                sp.dma_start(brow[n], ins[name][None, :]).then_inc(brow_loaded, 16)
            for n, (src, raw, _, _) in enumerate(pieces):
                sp.dma_start(raw, src).then_inc(w_loaded[n], 16)
            for k in range(TT):
                store_x1(0, 0, k)
                if k + 2 < TT:
                    load_tile(0, 0, k + 2)
            turns(sp, chunk)
            results(CPB - 1, 1)
            for s in out_stored:
                sp.wait_ge(s, 16 * B * CPB * TT // 2)

        @block.gpsimd
        def _(pool):
            with pool.Fori(0, B * CPB * TT) as g:
                pool.wait_ge(eps_done, g + 1)
                nc.gpsimd.tensor_tensor(rstd[:, :], var_eps[:, :], t.minus_half[:, :], ALU.pow).then_inc(rstd_done, 1)

        @block.tensor
        def _(pe):
            def project(i, b, k, first=False):
                g = TT * (2 * i + b) + k
                if not first:
                    pe.wait_ge(gated, g)
                pe.wait_ge(a_lo_done, g + 1)
                nc.tensor.matmul(proj_ps[:, :], ones_rows[:, :], bias_rows[:, 0, :], start=True, stop=False)
                for q in range(KT):
                    for n, (lhs, rhs) in enumerate(split_terms(a_hi[:, q, :], a_lo[:, q, :], wp_hi[:, q, :], wp_lo[:, q, :])):
                        last = nc.tensor.matmul(proj_ps[:, :], lhs, rhs, start=False, stop=(q == KT - 1 and n == 2))
                last.then_inc(proj_full, 1)

            def transposes(i, b, k, first=False):
                g = TT * (2 * i + b) + k
                pe.wait_ge(xn_done, g + 1)
                if not first:
                    pe.wait_ge(h32_done, g)
                for j in range(KT):
                    last = nc.tensor.transpose(tr_ps[:, j, :], xn[:, j * P:(j + 1) * P], t.ident[:, :])
                last.then_inc(turned, 1)

            def fc1(c, b, f):
                pe.wait_ge(f_free, FT * c + f + 1)
                for k in range(KT):
                    cols = slice(f * P, (f + 1) * P)
                    for n, (lhs, rhs) in enumerate(split_terms(w1_hi[:, k, cols], w1_lo[:, k, cols], hT_hi[b][:, k, :], hT_lo[b][:, k, :])):
                        last = nc.tensor.matmul(f_ps[f % 2][:, :], lhs, rhs, start=(k == 0 and n == 0), stop=(k == KT - 1 and n == 2))
                last.then_inc(f_full, 1)

            def fc2(c, f):
                pe.wait_ge(g_done, FT * c + f + 1 + 2)
                for k in range(TT):
                    if f == 0:
                        pe.wait_ge(acc_free, TT * c + k + 1)
                        nc.tensor.matmul(acc_ps[k][:, :], ones_rows[:, :], bias_rows[:, 1, :], start=True, stop=False)
                    tok = slice(k * P, (k + 1) * P)
                    for n, (lhs, rhs) in enumerate(split_terms(g_hi[f % GR][:, tok], g_lo[f % GR][:, tok], w2_hi[:, f, :], w2_lo[:, f, :])):
                        last = nc.tensor.matmul(acc_ps[k][:, :], lhs, rhs, start=False, stop=(f == FT - 1 and n == 2))
                    if f == FT - 1:
                        if k < TT - 1:
                            last.then_inc(acc_full, 1)
                        else:
                            last.then_inc(g_free, 1)
                if f < FT - 1:
                    last.then_inc(g_free, 1)

            def chunk(i, b, more, first):
                c = 2 * i + b
                pe.wait_ge(hT_done, TT * c + TT)
                for f in range(FT):
                    fc1(c, b, f)
                    if more and f % 4 == 0:
                        project(*nxt(i, b), f // 4)
                    if more and f % 4 == 2:
                        transposes(*nxt(i, b), f // 4)
                    if first and f == 1:
                        pe.wait_ge(w_lo_done, FC2_DONE)
                    if f >= 1:
                        fc2(c, f - 1)
                    elif not first:
                        fc2(c - 1, FT - 1)

            pe.wait_ge(brow_lo, 2)
            pe.wait_ge(w_lo_done, 1)
            project(0, 0, 0, True)
            for k in range(TT):
                if k < TT - 1:
                    project(0, 0, k + 1)
                transposes(0, 0, k, k == 0)
            pe.wait_ge(w_lo_done, FC1_DONE)
            turns(pe, chunk)
            fc2(B * CPB - 1, FT - 1)

        @block.scalar
        def _(act):
            def split_a(i, b, k, first=False):
                g = TT * (2 * i + b) + k
                act.wait_ge(a_loaded[k % 2], 16 * (2 * (2 * i + b) + k // 2) + 16)
                if not first:
                    act.wait_ge(proj_full, g)
                nc.scalar.activation(a_hi[:, :, :], a32[k % 2][:, :, :], ACT.Copy).then_inc(a_hi_done, 1)

            def modulate(i, b, k, first=False):
                g = TT * (2 * i + b) + k
                act.wait_ge(turned, g + 1)
                if not first:
                    act.wait_ge(hT_done, g)
                for j in range(KT):
                    last = nc.scalar.activation(h32[:, j, :], tr_ps[:, j, :], ACT.Identity,
                                                bias=t.mod_b[:, 1, b, j:j + 1], scale=t.mod_w[:, 1, b, j:j + 1])
                last.then_inc(h32_done, 1)

            def chunk(i, b, more, first):
                c = 2 * i + b
                for f in range(FT):
                    if more and f % 4 == 0:
                        split_a(*nxt(i, b), f // 4)
                    act.wait_ge(f_full, FT * c + f + 1)
                    act.wait_ge(g_done, FT * c + f + 1)
                    nc.scalar.activation(g32[f % 2][:, :], f_ps[f % 2][:, :], ACT.Gelu_apprx_tanh,
                                         bias=t.cols[:, R_FC1B + f:R_FC1B + f + 1]).then_inc(f_free, 1)
                    if more and f % 4 == 2:
                        modulate(*nxt(i, b), f // 4)

            def upper(n):
                act.wait_ge(w_loaded[n], 16)
                _, raw, hi, _ = pieces[n]
                nc.scalar.activation(hi, raw, ACT.Copy).then_inc(w_hi_done, 1)

            upper(0)
            split_a(0, 0, 0, True)
            for k in range(TT):
                if k < TT - 1:
                    upper(k + 1)
                    split_a(0, 0, k + 1)
                modulate(0, 0, k, k == 0)
            for n in range(TT, len(pieces)):
                upper(n)
            turns(act, chunk)

        @block.vector
        def _(dve):
            def lower_a(i, b, k):
                g = TT * (2 * i + b) + k
                dve.wait_ge(a_hi_done, g + 1)
                nc.vector.tensor_tensor(a_lo[:, :, :], a32[k % 2][:, :, :], a_hi[:, :, :].bitcast(F32), ALU.subtract).then_inc(a_lo_done, 1)

            def residual(i, b, k):
                g = TT * (2 * i + b) + k
                dve.wait_ge(proj_full, g + 1)
                dve.wait_ge(turned, g)
                nc.vector.tensor_tensor(proj[:, :], proj_ps[:, :], t.gates[:, 0, b, :], ALU.mult).then_inc(gated, 1)
                dve.wait_ge(gated, g + 1)
                dve.wait_ge(x_loaded[k % 2], 16 * (2 * (2 * i + b) + k // 2) + 16)
                nc.vector.tensor_tensor(xt[k % 2][:, :], proj[:, :], xt[k % 2][:, :], ALU.add).then_inc(x1_done, 1)
                dve.wait_ge(x1_done, g + 1)
                nc.vector.bn_stats(stats[:, :], xt[k % 2][:, :]).then_inc(stats_done, 1)
                dve.wait_ge(stats_done, g + 1)
                nc.vector.tensor_copy(t.scrap[:, 8:10], t.cols[:, 0:2])
                nc.vector.bn_aggr(mv[:, :], stats[:, :]).then_inc(mv_done, 1)
                dve.wait_ge(mv_done, g + 1)
                nc.vector.tensor_scalar(var_eps[:, :], mv[:, 1:2], LN_EPS, None, ALU.add).then_inc(eps_done, 1)

            def normalise(i, b, k):
                g = TT * (2 * i + b) + k
                dve.wait_ge(rstd_done, g + 1)
                nc.vector.tensor_scalar(xn[:, :], xt[k % 2][:, :], mv[:, 0:1], rstd[:, 0:1], ALU.subtract, ALU.mult).then_inc(xn_done, 1)

            def split_h(i, b, k):
                g = TT * (2 * i + b) + k
                tok = slice(k * P, (k + 1) * P)
                dve.wait_ge(h32_done, g + 1)
                nc.vector.tensor_copy(hT_hi[b][:, :, tok], h32[:, :, :]).then_inc(hT_hi_done, 1)
                dve.wait_ge(hT_hi_done, g + 1)
                nc.vector.tensor_tensor(hT_lo[b][:, :, tok], h32[:, :, :], hT_hi[b][:, :, tok].bitcast(F32), ALU.subtract).then_inc(hT_done, 1)

            def split_g(c, f):
                dve.wait_ge(f_free, FT * c + f + 1 + 2)
                dve.wait_ge(g_free, FT * c + f + 1)
                nc.vector.tensor_copy(g_hi[f % GR][:, :], g32[f % 2][:, :]).then_inc(g_hi_done, 1)
                dve.wait_ge(g_hi_done, FT * c + f + 1)
                nc.vector.tensor_tensor(g_lo[f % GR][:, :], g32[f % 2][:, :], g_hi[f % GR][:, :].bitcast(F32), ALU.subtract).then_inc(g_done, 1)

            def epilogue(i, b):
                c = 2 * i + b
                for k in range(TT):
                    if k < TT - 1:
                        dve.wait_ge(acc_full, (TT - 1) * c + k + 1)
                    else:
                        dve.wait_ge(g_free, FT * (c + 1) + GR)
                    nc.vector.tensor_tensor(acc_ps[k][:, :], acc_ps[k][:, :], t.gates[:, 1, b, :], ALU.mult).then_inc(acc_scaled, 1)
                    dve.wait_ge(acc_scaled, TT * c + k + 1)
                    dve.wait_ge(res_loaded[k % 2], 16 * (2 * c + k // 2) + 16)
                    nc.vector.tensor_tensor(res[k % 2][:, :], acc_ps[k][:, :], res[k % 2][:, :], ALU.add).then_inc(acc_free, 1)

            def chunk(i, b, more, first):
                c = 2 * i + b
                for f in range(FT):
                    if more and f % 4 == 0:
                        lower_a(*nxt(i, b), f // 4)
                    split_g(c, f)
                    if f == 0 and not first:
                        epilogue(*prv(i, b))
                    if more and f % 4 == 1:
                        residual(*nxt(i, b), f // 4)
                    if more and f % 4 == 2:
                        split_h(*nxt(i, b), f // 4)
                    if more and f % 4 == 1:
                        normalise(*nxt(i, b), f // 4)

            for free, (sem_, n) in enumerate(((f_free, 2), (g_done, 2), (g_free, GR), (acc_free, TT))):
                nc.vector.memset(t.scrap[:, free:free + 1], 0.0).then_inc(sem_, n)
            def lower(n):
                dve.wait_ge(w_hi_done, n + 1)
                _, raw, hi, lo = pieces[n]
                nc.vector.tensor_tensor(lo, raw, hi.bitcast(F32), ALU.subtract).then_inc(w_lo_done, 1)

            nc.vector.memset(bias_rows[:, :, :].bitcast(F32), 0.0).then_inc(rows_set, 1)
            nc.vector.memset(ones_rows[:, :].bitcast(F32), 1.0).then_inc(rows_set, 1)
            dve.wait_ge(brow_loaded, 32)
            dve.wait_ge(rows_set, 2)
            for n in range(2):
                nc.vector.tensor_copy(bias_rows[0:1, n, :], brow[n]).then_inc(brow_hi, 1)
            for n in range(2):
                dve.wait_ge(brow_hi, n + 1)
                nc.vector.tensor_tensor(bias_rows[32:33, n, :], brow[n], bias_rows[0:1, n, :].bitcast(F32),
                                        ALU.subtract).then_inc(brow_lo, 1)
            lower(0)
            lower_a(0, 0, 0)
            for k in range(TT):
                residual(0, 0, k)
                if k < TT - 1:
                    lower_a(0, 0, k + 1)
                normalise(0, 0, k)
                if k < TT - 1:
                    lower(k + 1)
                split_h(0, 0, k)
            for n in range(TT, len(pieces)):
                lower(n)
            turns(dve, chunk)
            epilogue(CPB - 1, 1)


class Shared:
    pass


def build(nc, ins, out):
    t = Shared()
    with ExitStack() as ctx:
        def sb(name, shape, dt=F32):
            return ctx.enter_context(nc.sbuf_tensor(name, shape, dt))

        t.qk_dram = nc.dram_tensor("qk_dram", [2, 2, NG, P, B, L], F32)
        t.v_dram = nc.dram_tensor("v_dram", [B, L, D], F32)
        t.a_dram = nc.dram_tensor("a_dram", [NG, P, B, L], F32)
        t.x1_dram = nc.dram_tensor("x1_dram", [B, L, D], F32)
        t.ident = sb("ident", [P, P])
        t.ones = sb("ones", [P, HD])
        t.minus_half = sb("minus_half", [P, 1])
        t.scrap = sb("scrap", [P, 10])
        t.cols = sb("cols", [P, N_ROWS])
        t.mod_w = sb("mod_w", [P, 2, B, KT])
        t.mod_b = sb("mod_b", [P, 2, B, KT])
        t.gates = sb("gates", [P, 2, B, D])
        with ExitStack() as early:
            t.wqkv_hi = early.enter_context(nc.sbuf_tensor("wqkv_hi", [P, KT, 3 * D], F32R))
            t.wqkv_raw, t.wqkv_lo = lower_half(nc, early, "wqkv_lo", [P, KT, 3 * D])
            t.v_bias = early.enter_context(nc.sbuf_tensor("v_bias", [P, D], F32))
            build_qkv(nc, t, ins)
        build_attention(nc, t)
        build_mlp(nc, t, ins, out)


_SHORT = {"x": "x", "cond_1024": "cond"} | {f"L0_cond_{n}": n for n in (
    "ln1_w", "ln1_b", "ln2_w", "ln2_b", "ada_w", "ada_b", "qkv_w", "qkv_b", "proj_w", "proj_b",
    "fc1_w", "fc1_b", "fc2_w", "fc2_b")}


def kernel(**inputs):
    import concourse.bacc as bacc
    from concourse.bass_utils import run_bass_kernel_spmd

    nc = bacc.Bacc("TRN2", target_bir_lowering=False, num_devices=1, dynamic_dma_scratch_size=1024)
    arrays, ins = {}, {}
    for name, short in _SHORT.items():
        a = np.ascontiguousarray(inputs[name])
        arrays[f"in_{short}"] = a
        ins[short] = nc.dram_tensor(f"in_{short}", a.shape, mybir.dt.from_np(a.dtype), kind="ExternalInput").ap()
    out = nc.dram_tensor("out_0", (B, L, D), F32, kind="ExternalOutput").ap()
    build(nc, ins, out)
    r = run_bass_kernel_spmd(nc, [arrays], core_ids=[0])
    return r.results[0]["out_0"]
```

```python
from contextlib import ExitStack

import numpy as np

import concourse.bass as bass
from concourse import mybir

F32 = mybir.dt.float32
F32R = mybir.dt.float32r
ALU = mybir.AluOpType
ACT = mybir.ActivationFunctionType
AX_X = mybir.AxisListType.X

P = 128
B, L, D = 2, 2048, 512
H, HD = 16, 32
FF = 4 * D
LN_EPS = 1e-5
KT = D // P
FT = FF // P
CH = 512
CPB = L // CH
TT = CH // P
HG = P // HD
NG = H // HG
NKT = L // P
SCALE = 1.0 / float(np.sqrt(np.float32(HD)))

R_LN1W, R_LN1B, R_LN2W, R_LN2B = 0, 4, 8, 12
R_ADAB = 16
R_QKB = 40
R_FC1B = 48
R_C = 64
N_ROWS = 72


def split_terms(a_hi, a_lo, b_hi, b_lo):
    return ((a_hi, b_hi), (a_hi, b_lo), (a_lo, b_hi))


def lower_half(nc, ctx, name, shape):
    with nc.sbuf_tensor(f"{name}_raw", shape, F32) as raw:
        pass
    return raw, ctx.enter_context(nc.sbuf_tensor(name, shape, F32R))


def build_qkv(nc, t, ins):
    NOUT = 2 * KT + TT
    NBANK = 6
    with ExitStack() as ctx:
        def sb(name, shape, dt=F32):
            return ctx.enter_context(nc.sbuf_tensor(name, shape, dt))

        def sem(name):
            return ctx.enter_context(nc.semaphore(name))

        rows = sb("rows", [N_ROWS, P])
        ada = sb("ada", [P, KT, 6 * D])
        expc = sb("expc", [P, B * KT])
        den = sb("den", [P, B * KT])
        rden = sb("rden", [P, B * KT])
        silu = sb("silu", [P, B, KT])
        silu_rep = sb("silu_rep", [P, B, KT, P])
        mod = sb("mod", [P, B, 16])
        tmp = sb("tmp", [P, 2, B, KT])
        adab = sb("adab", [P, 2, D])
        x_in = [sb(f"x_in{n}", [P, TT, D]) for n in range(2)]
        stats = sb("stats", [P, TT, 6])
        mv = sb("mv", [P, TT, 2])
        var_eps = sb("var_eps", [P, TT])
        rstd = sb("rstd", [P, TT])
        xn = [sb(f"xn{n}", [P, D]) for n in range(2)]
        h32 = [sb(f"h32_{n}", [P, KT, P]) for n in range(2)]
        hT_hi = [sb(f"hT_hi{n}", [P, KT, CH], F32R) for n in range(2)]
        hT_lo = [sb(f"hT_lo{n}", [P, KT, CH], F32R) for n in range(2)]
        qk_st = [sb(f"qk_st{n}", [P, 2, CH], F32R) for n in range(4)]
        v_st = [sb(f"v_st{n}", [P, TT, D]) for n in range(2)]
        tr_ps = [ctx.enter_context(nc.psum_tensor(f"tr_ps{n}", [P, KT, P], F32)) for n in range(2)]
        out_ps = [ctx.enter_context(nc.psum_tensor(f"out_ps{n}", [P, CH], F32)) for n in range(NBANK)]

        rows_loaded, bc_loaded, qkv_loaded = sem("rows_loaded"), sem("bc_loaded"), sem("qkv_loaded")
        ada_loaded = [sem(f"ada_loaded{n}") for n in range(2)]
        ident_zero, ident_done, consts_set = sem("ident_zero"), sem("ident_done"), sem("consts_set")
        rows_turned, cols_done, expc_done = sem("rows_turned"), sem("cols_done"), sem("expc_done")
        den_done, rden_done, silu_done, rep_done = sem("den_done"), sem("rden_done"), sem("silu_done"), sem("rep_done")
        mod_summed, mod_done, tmp_done, cols_mod = sem("mod_summed"), sem("mod_done"), sem("tmp_done"), sem("cols_mod")
        gates_done = sem("gates_done")
        w_hi_done, w_lo_done = sem("w_hi_done"), sem("w_lo_done")
        waits_passed = sem("waits_passed")
        x_loaded = [sem(f"x_loaded{n}") for n in range(2)]
        stats_done, mv_done, eps_done, rstd_done = sem("stats_done"), sem("mv_done"), sem("eps_done"), sem("rstd_done")
        xn_done, turned, h32_done, hT_hi_done, hT_done = sem("xn_done"), sem("turned"), sem("h32_done"), sem("hT_hi_done"), sem("hT_done")
        out_full, hi_done = sem("out_full"), sem("hi_done")
        out_free = sem("out_free")
        qk_stored = [sem(f"qk_stored{n}") for n in range(4)]
        v_stored = [sem(f"v_stored{n}") for n in range(2)]

        x_v = ins["x"].rearrange("b (t p) d -> b p t d", p=P)
        v_v = t.v_dram[:, :, :].rearrange("b (t p) d -> b p t d", p=P)
        block = ctx.enter_context(nc.Block())

        @block.sync
        def _(sp):
            def load_x(i, b, normalised=None):
                if normalised is not None:
                    sp.wait_ge(xn_done, normalised)
                    sp.sem_inc(waits_passed, 1)
                sp.dma_start(x_in[b][:, :, :], x_v[b, :, bass.ds(i * TT, TT), :]).then_inc(x_loaded[b], 16)

            def chunk(i, b, more):
                c = 2 * i + b
                if more:
                    load_x(i + 1, b, TT * c + TT)
                for m in range(2 * KT):
                    sp.wait_ge(out_free, NOUT * c + m + 1 + NBANK)
                    sp.sem_inc(waits_passed, 1)
                    sp.dma_start(t.qk_dram[m // KT, :, m % KT, :, b, bass.ds(i * CH, CH)].rearrange("s p t -> p s t"),
                                 qk_st[m % 4][:, :, :].bitcast(F32)).then_inc(qk_stored[m % 4], 16)
                sp.wait_ge(out_free, NOUT * c + NOUT + NBANK)
                sp.sem_inc(waits_passed, 1)
                sp.dma_start(v_v[b, :, bass.ds(i * TT, TT), :], v_st[b][:, :, :]).then_inc(v_stored[b], 16)

            for at, name in ((R_C, "cond"), (R_LN1W, "ln1_w"), (R_LN1B, "ln1_b"), (R_LN2W, "ln2_w"), (R_LN2B, "ln2_b"),
                             (R_ADAB, "ada_b"), (R_FC1B, "fc1_b"), (R_QKB, "qkv_b")):
                v = ins[name][0:2 * D] if name == "qkv_b" else ins[name]
                v = v.rearrange("b (r p) -> (b r) p", p=P) if name == "cond" else v.rearrange("(r p) -> r p", p=P)
                sp.dma_start(rows[at:at + v.shape[0], :], v).then_inc(rows_loaded, 16)
            ada_v = ins["ada_w"].rearrange("(k p) n -> p k n", p=P)
            sp.dma_start(ada[:, :, 0:2 * D], ada_v[:, :, 0:2 * D]).then_inc(ada_loaded[0], 16)
            sp.dma_start(t.v_bias[:, :], ins["qkv_b"][None, 2 * D:3 * D].to_broadcast([P, D])).then_inc(bc_loaded, 16)
            for n, g in enumerate((2, 5)):
                sp.dma_start(adab[:, n, :], ins["ada_b"][None, g * D:(g + 1) * D].to_broadcast([P, D])).then_inc(bc_loaded, 16)
            load_x(0, 1)
            sp.wait_ge(qkv_loaded, 16 * KT)
            sp.dma_start(ada[:, :, 2 * D:6 * D], ada_v[:, :, 2 * D:6 * D]).then_inc(ada_loaded[1], 16)
            with sp.Fori(0, CPB - 1) as i:
                chunk(i, 0, True)
                chunk(i, 1, True)
            chunk(CPB - 1, 0, False)
            chunk(CPB - 1, 1, False)
            for s in qk_stored:
                sp.wait_ge(s, 16 + 16 * 2 * B * CPB)
            for s in v_stored:
                sp.wait_ge(s, 16 + 16 * CPB)

        @block.gpsimd
        def _(pool):
            def rstds(c, k):
                pool.wait_ge(eps_done, TT * c + k + 1)
                nc.gpsimd.tensor_tensor(rstd[:, k:k + 1], var_eps[:, k:k + 1], t.minus_half[:, :], ALU.pow).then_inc(rstd_done, 1)

            nc.gpsimd.memset(t.ident[:, :], 0.0).then_inc(ident_zero, 1)
            nc.gpsimd.memset(t.minus_half[:, :], -0.5).then_inc(consts_set, 1)
            pool.wait_ge(ident_zero, 1)
            nc.gpsimd.affine_select(out=t.ident[:, :], in_=t.ident[:, :], compare_op=ALU.not_equal, fill=1.0, base=0,
                                    pattern=[[-1, P]], channel_multiplier=1).then_inc(ident_done, 1)
            nc.gpsimd.memset(t.ones[:, :], 1.0).then_inc(consts_set, 1)
            pool.wait_ge(consts_set, 2)
            with pool.Fori(0, B * CPB) as c:
                for k in range(TT):
                    rstds(c, k)

        @block.tensor
        def _(pe):
            def transposes(c, k, first=False):
                g = TT * c + k
                pe.wait_ge(xn_done, g + 1)
                if not first:
                    pe.wait_ge(h32_done, g - 1)
                for j in range(KT):
                    last = nc.tensor.transpose(tr_ps[k % 2][:, j, :], xn[k % 2][:, j * P:(j + 1) * P], t.ident[:, :])
                last.then_inc(turned, 1)

            def output(c, b, o):
                bank = out_ps[o % NBANK]
                pe.wait_ge(out_free, NOUT * c + o + 1)
                n = 0
                for k in range(KT):
                    h_hi, h_lo = hT_hi[b][:, k, :], hT_lo[b][:, k, :]
                    if o < 2 * KT:
                        cols = slice(o * P, (o + 1) * P)
                        pairs = split_terms(t.wqkv_hi[:, k, cols], t.wqkv_lo[:, k, cols], h_hi, h_lo)
                    else:
                        tok = slice((o - 2 * KT) * P, (o - 2 * KT + 1) * P)
                        pairs = split_terms(h_hi[:, tok], h_lo[:, tok], t.wqkv_hi[:, k, 2 * D:3 * D], t.wqkv_lo[:, k, 2 * D:3 * D])
                    for lhs, rhs in pairs:
                        last = nc.tensor.matmul(bank[:, :], lhs, rhs, start=(n == 0), stop=(n == 3 * KT - 1))
                        n += 1
                last.then_inc(out_full, 1)

            def columns(bank, n):
                for m in range(2 * KT):
                    at = 3 * n * D + m * P
                    for k in range(KT):
                        last = nc.tensor.matmul(bank[:, 2 * m:2 * m + 2], ada[:, k, at:at + P], silu[:, :, k],
                                                start=(k == 0), stop=(k == KT - 1))
                last.then_inc(mod_summed, 1)

            def gate(bank, n, b):
                at = (2, 5)[n] * D
                for k in range(KT):
                    last = nc.tensor.matmul(bank[:, :], silu_rep[:, b, k, :], ada[:, k, at:at + D],
                                            start=(k == 0), stop=(k == KT - 1))
                last.then_inc(out_full, 1)

            def chunk(i, b, more):
                c = 2 * i + b
                pe.wait_ge(hT_done, TT * c + TT)
                for k in range(TT):
                    output(c, b, 3 * k)
                    output(c, b, 3 * k + 1)
                    if more:
                        transposes(c + 1, k)
                    output(c, b, 3 * k + 2)

            pe.wait_ge(ident_done, 1)
            pe.wait_ge(rows_loaded, 16 * 8)
            nc.tensor.transpose(out_ps[0][:, 0:N_ROWS], rows[:, :], t.ident[0:N_ROWS, 0:N_ROWS]).then_inc(rows_turned, 1)
            transposes(0, 0, True)
            transposes(0, 1, True)
            pe.wait_ge(silu_done, 1)
            pe.wait_ge(ada_loaded[0], 16)
            columns(out_ps[1], 0)
            transposes(0, 2)
            transposes(0, 3)
            pe.wait_ge(w_lo_done, KT)
            with pe.Fori(0, CPB - 1) as i:
                chunk(i, 0, True)
                chunk(i, 1, True)
            chunk(CPB - 1, 0, True)
            chunk(CPB - 1, 1, False)
            pe.wait_ge(rep_done, B * KT)
            pe.wait_ge(ada_loaded[1], 16)
            for n in range(2 * B):
                pe.wait_ge(out_free, NOUT * B * CPB + n + 1)
                gate(out_ps[n % NBANK], n // B, n % B)
            pe.wait_ge(out_free, NOUT * B * CPB + 2 * B + 1)
            columns(out_ps[2 * B % NBANK], 1)

        @block.scalar
        def _(act):
            def modulate(c, b, k, first=False):
                g = TT * c + k
                act.wait_ge(turned, g + 1)
                if not first:
                    act.wait_ge(hT_done, g - 1)
                for j in range(KT):
                    last = nc.scalar.activation(h32[k % 2][:, j, :], tr_ps[k % 2][:, j, :], ACT.Identity,
                                                bias=t.mod_b[:, 0, b, j:j + 1], scale=t.mod_w[:, 0, b, j:j + 1])
                last.then_inc(h32_done, 1)

            def upper(c, b, o):
                act.wait_ge(out_full, NOUT * c + o + 1)
                act.wait_ge(qk_stored[o % 4], 16 * (2 * c + o // 4 + 1))
                nc.scalar.activation(qk_st[o % 4][:, 0, :], out_ps[o % NBANK][:, :], ACT.Identity,
                                     bias=t.cols[:, R_QKB + o:R_QKB + o + 1]).then_inc(hi_done, 1)

            def chunk(i, b, more):
                c = 2 * i + b
                for k in range(TT):
                    for o in (3 * k, 3 * k + 1):
                        if o < 2 * KT:
                            upper(c, b, o)
                    if more:
                        modulate(c + 1, 1 - b, k)
                    if 3 * k + 2 < 2 * KT:
                        upper(c, b, 3 * k + 2)

            x_view = x_v[0, :, 0:TT, :]
            act.dma_start(x_in[0][:, :, :], x_view).then_inc(x_loaded[0], 16)
            act.wait_ge(cols_done, 1)
            nc.scalar.activation(expc[:, :], t.cols[:, R_C:R_C + B * KT], ACT.Exp, scale=-1.0).then_inc(expc_done, 1)
            for k in range(KT):
                act.dma_start(t.wqkv_raw[:, k, :], ins["qkv_w"][k * P:(k + 1) * P, :]).then_inc(qkv_loaded, 16)
            act.wait_ge(qkv_loaded, 16 * KT)
            for k in range(KT):
                nc.scalar.activation(t.wqkv_hi[:, k, :], t.wqkv_raw[:, k, :], ACT.Copy).then_inc(w_hi_done, 1)
            act.wait_ge(cols_mod, 4)
            for k in range(TT):
                modulate(0, 0, k, k < 2)
            with act.Fori(0, CPB - 1) as i:
                chunk(i, 0, True)
                chunk(i, 1, True)
            chunk(CPB - 1, 0, True)
            chunk(CPB - 1, 1, False)

        @block.vector
        def _(dve):
            def tile_stats(i, b, k):
                g = TT * (2 * i + b) + k
                dve.wait_ge(x_loaded[b], 16 * i + 16)
                nc.vector.bn_stats(stats[:, k, :], x_in[b][:, k, :]).then_inc(stats_done, 1)
                dve.wait_ge(stats_done, g + 1)
                nc.vector.tensor_copy(t.scrap[:, 8:10], t.cols[:, 0:2])
                nc.vector.bn_aggr(mv[:, k, :], stats[:, k, :]).then_inc(mv_done, 1)
                dve.wait_ge(mv_done, g + 1)
                nc.vector.tensor_scalar(var_eps[:, k:k + 1], mv[:, k, 1:2], LN_EPS, None, ALU.add).then_inc(eps_done, 1)

            def normalise(i, b, k, first=False):
                g = TT * (2 * i + b) + k
                dve.wait_ge(rstd_done, g + 1)
                if not first:
                    dve.wait_ge(turned, g - 1)
                nc.vector.tensor_scalar(xn[k % 2][:, :], x_in[b][:, k, :], mv[:, k, 0:1], rstd[:, k:k + 1],
                                        ALU.subtract, ALU.mult).then_inc(xn_done, 1)

            def split_h(i, b, k):
                g = TT * (2 * i + b) + k
                tok = slice(k * P, (k + 1) * P)
                dve.wait_ge(h32_done, g + 1)
                nc.vector.tensor_copy(hT_hi[b][:, :, tok], h32[k % 2][:, :, :]).then_inc(hT_hi_done, 1)
                dve.wait_ge(hT_hi_done, g + 1)
                nc.vector.tensor_tensor(hT_lo[b][:, :, tok], h32[k % 2][:, :, :], hT_hi[b][:, :, tok].bitcast(F32),
                                        ALU.subtract).then_inc(hT_done, 1)

            def evacuate(i, b, o):
                c = 2 * i + b
                bank = out_ps[o % NBANK]
                if o < 2 * KT:
                    dve.wait_ge(hi_done, 2 * KT * c + o + 1)
                    nc.vector.scalar_tensor_tensor(qk_st[o % 4][:, 1, :], bank[:, :], t.cols[:, R_QKB + o:R_QKB + o + 1],
                                                   qk_st[o % 4][:, 0, :].bitcast(F32), ALU.add, ALU.subtract).then_inc(out_free, 1)
                else:
                    dve.wait_ge(out_full, NOUT * c + o + 1)
                    if o == 2 * KT:
                        dve.wait_ge(v_stored[b], 16 * i + 16)
                    nc.vector.tensor_tensor(v_st[b][:, o - 2 * KT, :], bank[:, :], t.v_bias[:, :], ALU.add).then_inc(out_free, 1)

            def chunk(i, b, more):
                ni, nb = (i, 1) if b == 0 else (i + 1, 0)
                for k in range(TT):
                    if more:
                        tile_stats(ni, nb, k)
                    evacuate(i, b, 3 * k)
                    if more:
                        normalise(ni, nb, k)
                    evacuate(i, b, 3 * k + 1)
                    if more:
                        split_h(ni, nb, k)
                    evacuate(i, b, 3 * k + 2)

            def modulation(bank, n):
                dve.wait_ge(mod_summed, n + 1)
                for b in range(B):
                    nc.vector.tensor_tensor(mod[:, b, 8 * n:8 * n + 8], bank[:, 0:4 * KT].rearrange("p (m b) -> p m b", b=B)[:, :, b],
                                            t.cols[:, R_ADAB + 12 * n:R_ADAB + 12 * n + 8], ALU.add).then_inc(mod_done, 1)
                dve.wait_ge(mod_done, 2 * n + 2)
                lw, lb = ((R_LN1W, R_LN1B), (R_LN2W, R_LN2B))[n]
                for b in range(B):
                    scale = mod[:, b, 8 * n + 4:8 * n + 8]
                    nc.vector.scalar_tensor_tensor(t.mod_w[:, n, b, :], scale, 1.0, t.cols[:, lw:lw + 4], ALU.add, ALU.mult).then_inc(cols_mod, 1)
                    nc.vector.scalar_tensor_tensor(tmp[:, n, b, :], scale, 1.0, t.cols[:, lb:lb + 4], ALU.add, ALU.mult).then_inc(tmp_done, 1)
                dve.wait_ge(tmp_done, 2 * n + 2)
                for b in range(B):
                    nc.vector.tensor_tensor(t.mod_b[:, n, b, :], tmp[:, n, b, :], mod[:, b, 8 * n:8 * n + 4], ALU.add).then_inc(cols_mod, 1)

            dve.wait_ge(rows_turned, 1)
            nc.vector.tensor_copy(t.cols[:, :], out_ps[0][:, 0:N_ROWS]).then_inc(cols_done, 1)
            dve.wait_ge(expc_done, 1)
            nc.vector.tensor_scalar(den[:, :], expc[:, :], 1.0, None, ALU.add).then_inc(den_done, 1)
            dve.wait_ge(den_done, 1)
            nc.vector.reciprocal(rden[:, :], den[:, :]).then_inc(rden_done, 1)
            dve.wait_ge(rden_done, 1)
            dve.wait_ge(cols_done, 1)
            nc.vector.tensor_tensor(silu[:, :, :], t.cols[:, R_C:R_C + B * KT].rearrange("p (b k) -> p b k", b=B),
                                    rden[:, :].rearrange("p (b k) -> p b k", b=B), ALU.mult).then_inc(silu_done, 1)
            for k in range(TT):
                tile_stats(0, 0, k)
            normalise(0, 0, 0, True)
            normalise(0, 0, 1, True)
            modulation(out_ps[1], 0)
            for k in range(KT):
                dve.wait_ge(w_hi_done, k + 1)
                nc.vector.tensor_tensor(t.wqkv_lo[:, k, :], t.wqkv_raw[:, k, :], t.wqkv_hi[:, k, :].bitcast(F32),
                                        ALU.subtract).then_inc(w_lo_done, 1)
            nc.vector.memset(t.scrap[:, 0:1], 0.0).then_inc(out_free, NBANK)
            for n, stored in enumerate(qk_stored + v_stored):
                nc.vector.memset(t.scrap[:, n + 1:n + 2], 0.0).then_inc(stored, 16)
            for k in range(TT):
                if k >= 2:
                    normalise(0, 0, k)
                split_h(0, 0, k)
            dve.wait_ge(silu_done, 1)
            for b in range(B):
                for k in range(KT):
                    nc.vector.tensor_copy(silu_rep[:, b, k, :], silu[:, b, k:k + 1].to_broadcast([P, P])).then_inc(rep_done, 1)
            dve.wait_ge(bc_loaded, 48)
            with dve.Fori(0, CPB - 1) as i:
                chunk(i, 0, True)
                chunk(i, 1, True)
            chunk(CPB - 1, 0, True)
            chunk(CPB - 1, 1, False)
            for n in range(2 * B):
                dve.wait_ge(out_full, NOUT * B * CPB + n + 1)
                nc.vector.tensor_tensor(t.gates[:, n // B, n % B, :], out_ps[n % NBANK][:, :], adab[:, n // B, :], ALU.add).then_inc(gates_done, 1)
            modulation(out_ps[2 * B % NBANK], 1)
            dve.wait_ge(gates_done, 2 * B)
            dve.wait_ge(cols_mod, 8)


def build_attention(nc, t):
    STEPS = 2 * CPB
    MX = HG * TT * CPB
    RING = 4
    AHEAD = 8
    LAG = 2
    TURN_AT = (MX - AHEAD) // HG
    PAIRS, QUADS = NKT // 2, NKT // 4
    BY_DVE, BY_POOL = (0,), (1,)
    QUAD_AT = {5: ((0, 0),), 6: ((0, 1),), 7: ((0, 2), (0, 3))}
    RECIP_AT, NORM_AT = 4, 8
    SUMS_AT = {8: (0,), 12: (2,), 14: (4,), NKT: (5,), NKT + 1: (6,), NKT + 2: (7,)}
    with ExitStack() as ctx:
        def sb(name, shape, dt=F32):
            return ctx.enter_context(nc.sbuf_tensor(name, shape, dt))

        def sem(name):
            return ctx.enter_context(nc.semaphore(name))

        ks = [sb(f"ks{n}", [3 * HD + 1, HG, L], F32R) for n in range(2)]
        qs = [sb(f"qs{n}", [3 * HD + 1, HG, CH], F32R) for n in range(CPB)]
        vs = [sb(f"vs{n}", [P, NKT, P]) for n in range(2)]
        prob = [sb(f"prob{n}", [P, HG, CH]) for n in range(RING)]
        pair = [sb(f"pair{n}", [P, HG, CH]) for n in range(4)]
        mpart = sb("mpart", [P, HG * TT, CPB])
        m16 = sb("m16", [P, HG * TT])
        mrow = sb("mrow", [HG * TT, P], F32R)
        o_sb = sb("o_sb", [P, CH])
        den_sb = sb("den_sb", [P, CH])
        den_flat = sb("den_flat", [P, HG * CH // P])
        rec_flat = sb("rec_flat", [P, HG * CH // P])
        rec = sb("rec", [P, CH])
        aT = [sb(f"aT{n}", [P, CH]) for n in range(2)]

        mx_ps = [ctx.enter_context(nc.psum_tensor(f"mx_ps{n}", [P, CH], F32)) for n in range(3)]
        s_ps = [ctx.enter_context(nc.psum_tensor(f"s_ps{n}", [P, CH], F32)) for n in range(3)]
        o_ps = ctx.enter_context(nc.psum_tensor("o_ps", [P, CH], F32))
        den_ps = ctx.enter_context(nc.psum_tensor("den_ps", [P, CH], F32))

        waits_passed = sem("waits_passed")
        k_loaded = [sem(f"k_loaded{n}") for n in range(2)]
        v_loaded = [sem(f"v_loaded{n}") for n in range(2)]
        q_loaded = [sem(f"q_loaded{n}") for n in range(CPB)]
        m_loaded = [sem(f"m_loaded{n}") for n in range(CPB)]
        ones_set = sem("ones_set")
        mx_full = sem("mx_full")
        mx_free = sem("mx_free")
        m16_done, m_turned, mrow_done = sem("m16_done"), sem("m_turned"), sem("mrow_done")
        s_full = sem("s_full")
        exp_done = sem("exp_done")
        prob_free = sem("prob_free")
        pair_done = sem("pair_done")
        quad_done, pool_quad_done = sem("quad_done"), sem("pool_quad_done")
        quad_free = sem("quad_free")
        o_copied = sem("o_copied")
        den_copied = sem("den_copied")
        den_spread, rec_stored, rec_loaded = sem("den_spread"), sem("rec_stored"), sem("rec_loaded")
        rec_done, norm_done = sem("rec_done"), sem("norm_done")
        a_stored = [sem(f"a_stored{n}") for n in range(2)]

        block = ctx.enter_context(nc.Block())
        v_v = t.v_dram[:, :, :].rearrange("b (t p) d -> b p t d", p=P)

        def bank(n, k):
            return (HG * NKT * n + k) % 3

        def turn_bank(n):
            return bank((n + 1) % STEPS, 2)

        def after(i, b, c, n=1):
            s = 4 * b + c + n
            return (i if s < STEPS else i + 1), (s // CPB) % 2, s % CPB

        @block.sync
        def _(sp):
            def load_kv(i, b, free=None):
                if free is not None:
                    sp.wait_ge(quad_free, free)
                    sp.sem_inc(waits_passed, 1)
                src = t.qk_dram[1, :, bass.ds(i, 1), :, b, :].rearrange("s o (j p) t -> (s o) p j t", p=HD)
                for at, half in enumerate((0, 0, 1)):
                    sp.dma_start(ks[b][at * HD:(at + 1) * HD, :, :].bitcast(F32), src[half]).then_inc(k_loaded[b], 16)
                sp.dma_start(vs[b][:, :, :], v_v[b, :, :, bass.ds(i * P, P)]).then_inc(v_loaded[b], 16)

            def load_q(i, b, c, used=None):
                if used is not None:
                    sp.wait_ge(s_full, used)
                    sp.sem_inc(waits_passed, 1)
                src = t.qk_dram[0, :, bass.ds(i, 1), :, b, c * CH:(c + 1) * CH].rearrange("s o (j p) t -> (s o) p j t", p=HD)
                for at, half in enumerate((0, 1, 0)):
                    sp.dma_start(qs[c][at * HD:(at + 1) * HD, :, :].bitcast(F32), src[half]).then_inc(q_loaded[c], 16)

            def store_max(s, c):
                sp.wait_ge(mrow_done, s + 1)
                sp.dma_start(qs[c][3 * HD:3 * HD + 1, :, :].bitcast(F32).rearrange("o j (q p) -> o (j q) p", p=P),
                             mrow[:, :].bitcast(F32)).then_inc(m_loaded[c], 16)

            def invert(s):
                sp.wait_ge(den_copied, s + 2)
                sp.sem_inc(waits_passed, 1)
                sp.dma_start(den_flat[:, :], den_sb[0:P:HD, :].rearrange("j (r q) -> j r q", r=HD)).then_inc(den_spread, 16)
                sp.wait_ge(rec_done, s + 1)
                sp.sem_inc(waits_passed, 1)
                sp.dma_start(t.rec_dram[:, :].rearrange("j (r q) -> (j r) q", r=HD), rec_flat[:, :]).then_inc(rec_stored, 16)
                sp.wait_ge(rec_stored, 16 * (s + 1))
                sp.sem_inc(waits_passed, 1)
                sp.dma_start(rec[:, :], t.rec_dram[:, None, :].to_broadcast([HG, HD, CH])).then_inc(rec_loaded, 16)

            def store_a(i, b, c, s):
                sp.wait_ge(norm_done, s + 2)
                sp.sem_inc(waits_passed, 1)
                sp.dma_start(t.a_dram[bass.ds(i, 1), :, b, c * CH:(c + 1) * CH].rearrange("o p t -> (o p) t"),
                             aT[c % 2][:, :]).then_inc(a_stored[c % 2], 16)

            def step(i, b, c, final, first):
                s = STEPS * i + 4 * b + c
                if not (final and 4 * b + c + 3 >= STEPS):
                    load_q(*after(i, b, c, 3), used=None if first else HG * NKT * s)
                if not first:
                    pi, pb, pc = (i, b, c - 1) if c else (i, 0, CPB - 1) if b else (i - 1, 1, CPB - 1)
                    invert(s - 1)
                    store_a(pi, pb, pc, s - 1)
                if c == 0 and not (final and b == 1):
                    load_kv(*after(i, b, 0, CPB)[:2], free=None if first else QUADS * s + 2)
                if not (final and 4 * b + c == STEPS - 1):
                    store_max(s + 1, (c + 1) % CPB)

            load_q(0, 0, 0)
            load_kv(0, 0)
            load_q(0, 0, 1)
            load_q(0, 0, 2)
            store_max(0, 0)
            for n in range(STEPS):
                step(0, n // CPB, n % CPB, False, n == 0)
            with sp.Fori(1, NG - 1) as i:
                for n in range(STEPS):
                    step(i, n // CPB, n % CPB, False, False)
            for n in range(STEPS):
                step(NG - 1, n // CPB, n % CPB, True, False)
            invert(NG * STEPS - 1)
            store_a(NG - 1, 1, CPB - 1, NG * STEPS - 1)
            for s in a_stored:
                sp.wait_ge(s, 16 * NG * STEPS // 2)

        @block.gpsimd
        def _(pool):
            with pool.Fori(0, NG) as i:
                for n in range(STEPS):
                    s = STEPS * i + n
                    for p in range(PAIRS):
                        if p % 2 == 0:
                            pool.wait_ge(quad_free, QUADS * s + p // 2 + 1)
                        for j in range(HG):
                            pool.wait_ge(exp_done, HG * (NKT * s + 2 * p + 1) + j + 1 + 3)
                            nc.gpsimd.tensor_tensor(pair[p % 4][:, j, :], prob[2 * p % RING][:, j, :],
                                                    prob[(2 * p + 1) % RING][:, j, :], ALU.add).then_inc(pair_done, 1)
                        if p % 2 == 1 and p // 2 in BY_POOL:
                            even, odd = pair[(p - 1) % 4], pair[p % 4]
                            for j in range(HG):
                                pool.wait_ge(pair_done, HG * (PAIRS * s + p) + j + 1)
                                nc.gpsimd.tensor_tensor(even[:, j, :], even[:, j, :], odd[:, j, :], ALU.add).then_inc(pool_quad_done, 1)

        @block.tensor
        def _(pe):
            def max_slot(s, b, c, k, first=False):
                j, q, quarter = k // (TT * CPB), k // CPB % TT, k % CPB
                if k == 2:
                    pe.wait_ge(mrow_done, s)
                elif k < 2 and b == 0 and c == 0 and not first:
                    pe.wait_ge(mx_free, 2 * MX * s + 2 * k + 4)
                else:
                    pe.wait_ge(mx_free, 2 * MX * s + 2 * k + 2)
                nc.tensor.matmul(mx_ps[bank(CPB * b + c, k)][:, :], qs[c][0:3 * HD, j, q * P:(q + 1) * P],
                                 ks[b][0:3 * HD, j, quarter * CH:(quarter + 1) * CH], start=True, stop=True).then_inc(mx_full, 1)

            def turn_max(s, n):
                pe.wait_ge(m16_done, s + 1)
                nc.tensor.transpose(mx_ps[turn_bank(n)][0:HG * TT, 0:P], m16[:, :], t.ident[:, :]).then_inc(m_turned, 1)

            def max_begin(i, b, c, k, first=False):
                s = STEPS * i + 4 * b + c
                if k == 0:
                    pe.wait_ge(q_loaded[c], 48 * (2 * i + b) + 48)
                if k == 0 and c == 0:
                    pe.wait_ge(k_loaded[b], 48 * i + 48)
                max_slot(s, b, c, k, first)

            def score(s, b, c, kt, j, first=False):
                k = HG * kt + j
                if b == 0 and c == 0 and k < 2 and not first:
                    pe.wait_ge(exp_done, HG * NKT * s + k + 2)
                else:
                    pe.wait_ge(exp_done, HG * NKT * s + k + 1)
                nc.tensor.matmul(s_ps[bank(CPB * b + c, k)][:, :], ks[b][:, j, kt * P:(kt + 1) * P], qs[c][:, j, :],
                                 start=True, stop=True).then_inc(s_full, 1)

            def values(s, b, kt):
                if kt == 0:
                    pe.wait_ge(o_copied, s + 1)
                pe.wait_ge(exp_done, HG * (NKT * s + kt + 1) + 3)
                for j in range(HG):
                    last = nc.tensor.matmul(o_ps[j * HD:(j + 1) * HD, :], vs[b][:, kt, j * HD:(j + 1) * HD],
                                            prob[kt % RING][:, j, :], start=(kt == 0), stop=(kt == NKT - 1))
                last.then_inc(prob_free, 1)

            def key_sums(s, p):
                g = p // 2
                if g in BY_DVE:
                    pe.wait_ge(quad_done, HG * (len(BY_DVE) * s + BY_DVE.index(g) + 1))
                elif g in BY_POOL:
                    pe.wait_ge(pool_quad_done, HG * (len(BY_POOL) * s + BY_POOL.index(g) + 1))
                else:
                    pe.wait_ge(pair_done, HG * (PAIRS * s + p + 1))
                if p == 0:
                    pe.wait_ge(den_copied, s + 1)
                for j in range(HG):
                    last = nc.tensor.matmul(den_ps[j * HD:(j + 1) * HD, :], t.ones[:, 0:HD], pair[p % 4][:, j, :],
                                            start=(p == 0), stop=(p == PAIRS - 1))
                if g in BY_DVE + BY_POOL or p % 2 == 1:
                    last.then_inc(quad_free, 1)

            def step(i, b, c, final, first):
                n = 4 * b + c
                s = STEPS * i + n
                ni, nb, ncx = after(i, b, c)
                with_max = not (final and n == STEPS - 1)
                begin_max = not (final and n >= STEPS - 2)
                pe.wait_ge(m_loaded[c], 16 * (2 * i + b) + 16)
                if c == 0:
                    pe.wait_ge(v_loaded[b], 16 * i + 16)
                for kt in range(NKT):
                    def maximum(j):
                        if with_max and kt < TURN_AT:
                            max_slot(s + 1, nb, ncx, AHEAD + HG * kt + j)
                        elif begin_max and kt >= TURN_AT:
                            max_begin(*after(i, b, c, 2), HG * (kt - TURN_AT) + j)

                    score(s, b, c, kt, 0, first)
                    maximum(0)
                    if kt >= LAG:
                        values(s, b, kt - LAG)
                    elif not first:
                        values(s - 1, (n - 1) // CPB % 2, NKT - LAG + kt)
                    score(s, b, c, kt, 1, first)
                    maximum(1)
                    score(s, b, c, kt, 2)
                    if with_max and kt == TURN_AT:
                        turn_max(s + 1, (n + 1) % STEPS)
                    else:
                        maximum(2)
                    score(s, b, c, kt, 3)
                    for p in SUMS_AT.get(kt, ()):
                        key_sums(s, p)
                    if not first:
                        for p in SUMS_AT.get(NKT + kt, ()):
                            key_sums(s - 1, p)
                    if with_max and kt == TURN_AT:
                        maximum(2)
                    maximum(3)

            pe.wait_ge(ones_set, 2)
            max_begin(0, 0, 0, 0, True)
            for k in range(1, MX):
                max_slot(0, 0, 0, k, True)
            turn_max(0, 0)
            for k in range(AHEAD):
                max_begin(0, 0, 1, k)
            for n in range(STEPS):
                step(0, n // CPB, n % CPB, False, n == 0)
            with pe.Fori(1, NG - 1) as i:
                for n in range(STEPS):
                    step(i, n // CPB, n % CPB, False, False)
            for n in range(STEPS):
                step(NG - 1, n // CPB, n % CPB, True, False)
            s = NG * STEPS - 1
            for kt in range(NKT - LAG, NKT):
                values(s, 1, kt)
            for p in range(PAIRS):
                if any(p in SUMS_AT.get(kt, ()) for kt in range(NKT, 2 * NKT)):
                    key_sums(s, p)

        @block.scalar
        def _(act):
            def exponential(s, n, kt, j, first):
                act.wait_ge(s_full, HG * (NKT * s + kt) + j + 1)
                act.wait_ge(prob_free, NKT * s + kt + 1)
                if kt >= RING or not first:
                    act.wait_ge(pair_done, HG * (PAIRS * s + (kt - RING) // 2) + j + 1)
                nc.scalar.activation(prob[kt % RING][:, j, :], s_ps[bank(n, HG * kt + j)][:, :], ACT.Exp, scale=SCALE).then_inc(exp_done, 1)

            def copy_outputs(s):
                act.wait_ge(prob_free, NKT * (s + 1) + RING)
                act.wait_ge(norm_done, s + 1)
                nc.scalar.activation(o_sb[:, :], o_ps[:, :], ACT.Copy).then_inc(o_copied, 1)

            def copy_denominators(s):
                act.wait_ge(quad_free, QUADS * (s + 1) + 2)
                act.wait_ge(norm_done, s + 1)
                nc.scalar.activation(den_sb[:, :], den_ps[:, :], ACT.Copy).then_inc(den_copied, 1)

            def step(i, n, first):
                s = STEPS * i + n
                for kt in range(NKT):
                    for j in range(HG):
                        exponential(s, n, kt, j, first)
                        if kt == LAG - 1 and j == 1 and not first:
                            copy_outputs(s - 1)
                        if kt == 3 and j == 1 and not first:
                            copy_denominators(s - 1)

            for n in range(STEPS):
                step(0, n, n == 0)
            with act.Fori(1, NG) as i:
                for n in range(STEPS):
                    step(i, n, False)
            copy_outputs(NG * STEPS - 1)
            copy_denominators(NG * STEPS - 1)

        @block.vector
        def _(dve):
            def maxima(s, n, k):
                dve.wait_ge(mx_full, MX * s + k + 1)
                nc.vector.tensor_reduce(mpart[:, k // CPB, k % CPB:k % CPB + 1], mx_ps[bank(n, k)][:, :], AX_X, ALU.max).then_inc(mx_free, 2)

            def combine(s):
                dve.wait_ge(mx_free, 2 * MX * (s + 1) + 6)
                nc.vector.tensor_reduce(m16[:, :], mpart[:, :, :], AX_X, ALU.max).then_inc(m16_done, 1)

            def negate(s, n):
                dve.wait_ge(m_turned, s + 1)
                nc.vector.tensor_scalar(mrow[:, :], mx_ps[turn_bank(n)][0:HG * TT, 0:P], -1.0, None, ALU.mult).then_inc(mrow_done, 1)

            def add_pairs(s, g, j):
                dve.wait_ge(pair_done, HG * (PAIRS * s + 2 * g + 1) + j + 1)
                even, odd = pair[2 * g % 4], pair[(2 * g + 1) % 4]
                nc.vector.tensor_tensor(even[:, j, :], even[:, j, :], odd[:, j, :], ALU.add).then_inc(quad_done, 1)

            def reciprocals(s):
                dve.wait_ge(den_spread, 16 * (s + 1))
                nc.vector.reciprocal(rec_flat[:, :], den_flat[:, :]).then_inc(rec_done, 1)

            def normalise(s, c, stored):
                dve.wait_ge(rec_loaded, 16 * (s + 1))
                dve.wait_ge(o_copied, s + 2)
                dve.wait_ge(a_stored[c % 2], stored)
                nc.vector.tensor_tensor(aT[c % 2][:, :], o_sb[:, :], rec[:, :], ALU.mult).then_inc(norm_done, 1)

            def step(i, b, c, final, first):
                n = 4 * b + c
                s = STEPS * i + n
                with_max = not (final and n == STEPS - 1)
                begin_max = not (final and n >= STEPS - 2)
                for kt in range(NKT):
                    if with_max and kt < TURN_AT:
                        for j in range(HG):
                            maxima(s + 1, (n + 1) % STEPS, AHEAD + HG * kt + j)
                    if with_max and kt == TURN_AT:
                        combine(s + 1)
                        dve.wait_ge(m_loaded[c], 16 * (2 * i + b) + 16)
                        negate(s + 1, (n + 1) % STEPS)
                    if begin_max and kt >= TURN_AT:
                        for j in range(HG):
                            maxima(s + 2, (n + 2) % STEPS, HG * (kt - TURN_AT) + j)
                    for g, j in QUAD_AT.get(kt, ()):
                        add_pairs(s, g, j)
                    if not first:
                        if kt == RECIP_AT:
                            reciprocals(s - 1)
                        if kt == NORM_AT:
                            normalise(s - 1, (c - 1) % CPB, 16 * (4 * i + (n - 1) // 2) if n else 16 * (4 * i - 1))

            for free, (sem_, n) in enumerate(((mx_free, 6), (exp_done, 3), (prob_free, RING), (quad_free, 2), (o_copied, 1), (den_copied, 1), (norm_done, 1))):
                nc.vector.memset(t.scrap[:, free:free + 1], 0.0).then_inc(sem_, n)
            for b in range(2):
                nc.vector.memset(ks[b][3 * HD:3 * HD + 1, :, :].bitcast(F32), 1.0).then_inc(ones_set, 1)
            for k in range(MX):
                maxima(0, 0, k)
            combine(0)
            negate(0, 0)
            for k in range(AHEAD):
                maxima(1, 1, k)
            for n in range(STEPS):
                step(0, n // CPB, n % CPB, False, n == 0)
            with dve.Fori(1, NG - 1) as i:
                for n in range(STEPS):
                    step(i, n // CPB, n % CPB, False, False)
            for n in range(STEPS):
                step(NG - 1, n // CPB, n % CPB, True, False)
            s = NG * STEPS - 1
            reciprocals(s)
            normalise(s, CPB - 1, 16 * (s // 2))


def build_mlp(nc, t, ins, out):
    GR = 2
    with ExitStack() as ctx:
        def sb(name, shape, dt=F32):
            return ctx.enter_context(nc.sbuf_tensor(name, shape, dt))

        def sem(name):
            return ctx.enter_context(nc.semaphore(name))

        wp_hi, w1_hi, w2_hi = sb("wp_hi", [P, KT, D], F32R), sb("w1_hi", [P, KT, FF], F32R), sb("w2_hi", [P, FT, D], F32R)
        wp_raw, wp_lo = lower_half(nc, ctx, "wp_lo", [P, KT, D])
        w1_raw, w1_lo = lower_half(nc, ctx, "w1_lo", [P, KT, FF])
        w2_raw, w2_lo = lower_half(nc, ctx, "w2_lo", [P, FT, D])
        bias_rows = sb("bias_rows", [3 * HD + 1, D], F32R)
        pick_rows = sb("pick_rows", [3 * HD + 1, 2, P], F32R)
        hT_hi = [sb(f"h2_hi{n}", [P, KT, CH], F32R) for n in range(2)]
        hT_lo = [sb(f"h2_lo{n}", [P, KT, CH], F32R) for n in range(2)]
        a32, a_lo = zip(*(lower_half(nc, ctx, f"a_lo{n}", [P, KT, P]) for n in range(2)))
        a_hi = sb("a_hi", [P, KT, P], F32R)
        xt = [sb(f"xt{n}", [P, D]) for n in range(2)]
        stats = sb("stats2", [P, 6])
        mv = sb("mv2", [P, 2])
        var_eps = sb("var_eps2", [P, 1])
        rstd = sb("rstd2", [P, 1])
        proj = sb("proj", [P, D])
        xn = proj
        h32 = sb("h32m", [P, KT, P])
        g32 = [sb(f"g32_{n}", [P, CH]) for n in range(2)]
        brow = [g32[n][64 * n:64 * n + 1, :] for n in range(2)]
        g_hi = [sb(f"g_hi{n}", [P, CH], F32R) for n in range(GR)]
        g_lo = [sb(f"g_lo{n}", [P, CH], F32R) for n in range(GR)]
        res = [sb(f"res{n}", [P, D]) for n in range(TT)]
        acc_ps = [ctx.enter_context(nc.psum_tensor(f"acc_ps{n}", [P, D], F32)) for n in range(TT)]
        f_ps = [ctx.enter_context(nc.psum_tensor(f"f_ps{n}", [P, CH], F32)) for n in range(2)]
        proj_ps = ctx.enter_context(nc.psum_tensor("proj_ps", [P, D], F32))
        tr_ps = ctx.enter_context(nc.psum_tensor("tr2_ps", [P, KT, P], F32))

        FC1_DONE, FC2_DONE = 1 + KT, 1 + 2 * KT
        fc2_v = ins["fc2_w"].rearrange("(k p) n -> p k n", p=P)
        pieces = [(ins["proj_w"].rearrange("(k p) n -> p k n", p=P), wp_raw[:, :, :], wp_hi[:, :, :], wp_lo[:, :, :])]
        pieces += [(ins["fc1_w"][k * P:(k + 1) * P, :], w1_raw[:, k, :], w1_hi[:, k, :], w1_lo[:, k, :]) for k in range(KT)]
        pieces += [(fc2_v[:, k:k + KT, :], w2_raw[:, k:k + KT, :], w2_hi[:, k:k + KT, :],
                    w2_lo[:, k:k + KT, :]) for k in range(0, FT, KT)]

        w_loaded = [sem(f"w_loaded{n}") for n in range(len(pieces))]
        w_hi_done, w_lo_done = sem("w2_hi_done"), sem("w2_lo_done")
        brow_loaded, rows_set, brow_hi, brow_lo = sem("brow_loaded"), sem("rows_set"), sem("brow_hi"), sem("brow_lo")
        waits_passed = sem("waits_passed")
        a_loaded = [sem(f"a_loaded{n}") for n in range(2)]
        x_loaded = [sem(f"xt_loaded{n}") for n in range(2)]
        a_hi_done, a_lo_done, proj_full, gated = sem("a_hi_done"), sem("a_lo_done"), sem("proj_full"), sem("gated")
        x1_done, stats_done, mv_done, eps_done, rstd_done = (sem("x1_done"), sem("stats2_done"), sem("mv2_done"),
                                                             sem("eps2_done"), sem("rstd2_done"))
        x1_stored = [sem(f"x1_stored{n}") for n in range(2)]
        xn_done, turned, h32_done, hT_hi_done, hT_done = (sem("xn2_done"), sem("turned2"), sem("h32m_done"),
                                                          sem("h2_hi_done"), sem("h2_done"))
        f_full = sem("f_full")
        f_free = sem("f_free")
        g_hi_done = sem("g_hi_done")
        g_done = sem("g_done")
        g_free = sem("g_free")
        acc_full = sem("acc_full")
        acc_free = sem("acc_free")
        acc_scaled = sem("acc_scaled")
        res_loaded = [sem(f"res_loaded{n}") for n in range(TT)]
        out_stored = [sem(f"out_stored{n}") for n in range(TT)]

        x_v = ins["x"].rearrange("b (t p) d -> b t p d", p=P)
        x1_v = t.x1_dram[:, :, :].rearrange("b (t p) d -> b t p d", p=P)
        out_v = out.rearrange("b (t p) d -> b t p d", p=P)
        block = ctx.enter_context(nc.Block())

        def nxt(i, b):
            return (i, 1) if b == 0 else (i + 1, 0)

        def prv(i, b):
            return (i, 0) if b == 1 else (i - 1, 1)

        def turns(eng, chunk):
            chunk(0, 0, True, True)
            chunk(0, 1, True, False)
            with eng.Fori(1, CPB - 1) as i:
                chunk(i, 0, True, False)
                chunk(i, 1, True, False)
            chunk(CPB - 1, 0, True, False)
            chunk(CPB - 1, 1, False, False)

        @block.sync
        def _(sp):
            def load_tile(i, b, k, first=False):
                c = 2 * i + b
                if not first:
                    sp.wait_ge(proj_full, TT * c + k - 1)
                    sp.sem_inc(waits_passed, 1)
                    sp.wait_ge(x1_stored[k % 2], 16 * (2 * c + k // 2))
                    sp.sem_inc(waits_passed, 1)
                    sp.wait_ge(xn_done, TT * c + k - 1)
                    sp.sem_inc(waits_passed, 1)
                sp.dma_start(a32[k % 2][:, :, :], t.a_dram[:, :, b, bass.ds(i * CH + k * P, P)].rearrange("g p t -> p g t")
                             ).then_inc(a_loaded[k % 2], 16)
                sp.dma_start(xt[k % 2][:, :], x_v[b, bass.ds(i * TT + k, 1), :, :].rearrange("o p d -> (o p) d")
                             ).then_inc(x_loaded[k % 2], 16)

            def store_x1(i, b, k):
                sp.wait_ge(x1_done, TT * (2 * i + b) + k + 1)
                sp.sem_inc(waits_passed, 1)
                sp.dma_start(x1_v[b, bass.ds(i * TT + k, 1), :, :].rearrange("o p d -> (o p) d"), xt[k % 2][:, :]
                             ).then_inc(x1_stored[k % 2], 16)

            def load_res(i, b, k, first=False):
                c = 2 * i + b
                if not first:
                    sp.wait_ge(out_stored[k], 16 * c)
                    sp.sem_inc(waits_passed, 1)
                sp.wait_ge(x1_stored[k % 2], 16 * (2 * c + k // 2) + 16)
                sp.sem_inc(waits_passed, 1)
                sp.dma_start(res[k][:, :], x1_v[b, bass.ds(i * TT + k, 1), :, :].rearrange("o p d -> (o p) d")
                             ).then_inc(res_loaded[k], 16)

            def store_out(i, b, k):
                sp.wait_ge(acc_free, TT * (2 * i + b) + k + 1 + TT)
                sp.sem_inc(waits_passed, 1)
                sp.dma_start(out_v[b, bass.ds(i * TT + k, 1), :, :].rearrange("o p d -> (o p) d"), res[k][:, :]
                             ).then_inc(out_stored[k], 16)

            def chunk(i, b, more, first):
                ni, nb = nxt(i, b)
                if more:
                    load_tile(ni, nb, 0)
                    load_tile(ni, nb, 1)
                for k in range(TT):
                    if not first:
                        store_out(*prv(i, b), k)
                for k in range(TT):
                    load_res(i, b, k, first)
                if more:
                    for k in range(TT):
                        store_x1(ni, nb, k)
                        if k + 2 < TT:
                            load_tile(ni, nb, k + 2)

            load_tile(0, 0, 0, True)
            load_tile(0, 0, 1, True)
            for n, name in enumerate(("proj_b", "fc2_b")):
                sp.dma_start(brow[n], ins[name][None, :]).then_inc(brow_loaded, 16)
            for n, (src, raw, _, _) in enumerate(pieces[:FC1_DONE]):
                sp.dma_start(raw, src).then_inc(w_loaded[n], 16)
            for k in range(TT):
                store_x1(0, 0, k)
                if k + 2 < TT:
                    load_tile(0, 0, k + 2)
            turns(sp, chunk)
            for k in range(TT):
                store_out(CPB - 1, 1, k)
            for s in out_stored:
                sp.wait_ge(s, 16 * B * CPB)

        @block.gpsimd
        def _(pool):
            with pool.Fori(0, B * CPB * TT) as g:
                pool.wait_ge(eps_done, g + 1)
                nc.gpsimd.tensor_tensor(rstd[:, :], var_eps[:, :], t.minus_half[:, :], ALU.pow).then_inc(rstd_done, 1)

        @block.tensor
        def _(pe):
            def project(i, b, k, first=False):
                g = TT * (2 * i + b) + k
                if not first:
                    pe.wait_ge(gated, g)
                pe.wait_ge(a_lo_done, g + 1)
                nc.tensor.matmul(proj_ps[:, :], pick_rows[:, 0, :], bias_rows[:, :], start=True, stop=False)
                for q in range(KT):
                    for n, (lhs, rhs) in enumerate(split_terms(a_hi[:, q, :], a_lo[k % 2][:, q, :], wp_hi[:, q, :], wp_lo[:, q, :])):
                        last = nc.tensor.matmul(proj_ps[:, :], lhs, rhs, start=False, stop=(q == KT - 1 and n == 2))
                last.then_inc(proj_full, 1)

            def transposes(i, b, k, first=False):
                g = TT * (2 * i + b) + k
                pe.wait_ge(xn_done, g + 1)
                if not first:
                    pe.wait_ge(h32_done, g)
                for j in range(KT):
                    last = nc.tensor.transpose(tr_ps[:, j, :], xn[:, j * P:(j + 1) * P], t.ident[:, :])
                last.then_inc(turned, 1)

            def fc1(c, b, f):
                pe.wait_ge(f_free, FT * c + f + 1)
                for k in range(KT):
                    cols = slice(f * P, (f + 1) * P)
                    for n, (lhs, rhs) in enumerate(split_terms(w1_hi[:, k, cols], w1_lo[:, k, cols], hT_hi[b][:, k, :], hT_lo[b][:, k, :])):
                        last = nc.tensor.matmul(f_ps[f % 2][:, :], lhs, rhs, start=(k == 0 and n == 0), stop=(k == KT - 1 and n == 2))
                last.then_inc(f_full, 1)

            def fc2(c, f):
                pe.wait_ge(g_done, FT * c + f + 1 + 2)
                for k in range(TT):
                    if f == 0:
                        pe.wait_ge(acc_free, TT * c + k + 1)
                        nc.tensor.matmul(acc_ps[k][:, :], pick_rows[:, 1, :], bias_rows[:, :], start=True, stop=False)
                    tok = slice(k * P, (k + 1) * P)
                    for n, (lhs, rhs) in enumerate(split_terms(g_hi[f % GR][:, tok], g_lo[f % GR][:, tok], w2_hi[:, f, :], w2_lo[:, f, :])):
                        last = nc.tensor.matmul(acc_ps[k][:, :], lhs, rhs, start=False, stop=(f == FT - 1 and n == 2))
                    if f == FT - 1:
                        if k < TT - 1:
                            last.then_inc(acc_full, 1)
                        else:
                            last.then_inc(g_free, 1)
                if f < FT - 1:
                    last.then_inc(g_free, 1)

            def chunk(i, b, more, first):
                c = 2 * i + b
                pe.wait_ge(hT_done, TT * c + TT)
                for f in range(FT):
                    fc1(c, b, f)
                    if more and f % 4 == 0:
                        project(*nxt(i, b), f // 4)
                    if more and f % 4 == 2:
                        transposes(*nxt(i, b), f // 4)
                    if first and f == 1:
                        pe.wait_ge(w_lo_done, FC2_DONE)
                    if f >= 1:
                        fc2(c, f - 1)
                    elif not first:
                        fc2(c - 1, FT - 1)

            pe.wait_ge(rows_set, 4)
            pe.wait_ge(brow_lo, 2)
            pe.wait_ge(w_lo_done, 1)
            project(0, 0, 0, True)
            for k in range(TT):
                if k < TT - 1:
                    project(0, 0, k + 1)
                transposes(0, 0, k, k == 0)
            pe.wait_ge(w_lo_done, FC1_DONE)
            turns(pe, chunk)
            fc2(B * CPB - 1, FT - 1)

        @block.scalar
        def _(act):
            def split_a(i, b, k, first=False):
                g = TT * (2 * i + b) + k
                act.wait_ge(a_loaded[k % 2], 16 * (2 * (2 * i + b) + k // 2) + 16)
                if not first:
                    act.wait_ge(proj_full, g)
                nc.scalar.activation(a_hi[:, :, :], a32[k % 2][:, :, :], ACT.Copy).then_inc(a_hi_done, 1)

            def modulate(i, b, k, first=False):
                g = TT * (2 * i + b) + k
                act.wait_ge(turned, g + 1)
                if not first:
                    act.wait_ge(hT_done, g)
                for j in range(KT):
                    last = nc.scalar.activation(h32[:, j, :], tr_ps[:, j, :], ACT.Identity,
                                                bias=t.mod_b[:, 1, b, j:j + 1], scale=t.mod_w[:, 1, b, j:j + 1])
                last.then_inc(h32_done, 1)

            def chunk(i, b, more, first):
                c = 2 * i + b
                for f in range(FT):
                    if more and f % 4 == 0:
                        split_a(*nxt(i, b), f // 4)
                    act.wait_ge(f_full, FT * c + f + 1)
                    act.wait_ge(g_done, FT * c + f + 1)
                    nc.scalar.activation(g32[f % 2][:, :], f_ps[f % 2][:, :], ACT.Gelu_apprx_tanh,
                                         bias=t.cols[:, R_FC1B + f:R_FC1B + f + 1]).then_inc(f_free, 1)
                    if more and f % 4 == 2:
                        modulate(*nxt(i, b), f // 4)

            def upper(n):
                act.wait_ge(w_loaded[n], 16)
                _, raw, hi, _ = pieces[n]
                nc.scalar.activation(hi, raw, ACT.Copy).then_inc(w_hi_done, 1)

            upper(0)
            split_a(0, 0, 0, True)
            for k in range(TT):
                if k < TT - 1:
                    upper(k + 1)
                    split_a(0, 0, k + 1)
                if k == 1:
                    for m in range(FC1_DONE, FC2_DONE):
                        act.dma_start(pieces[m][1], pieces[m][0]).then_inc(w_loaded[m], 16)
                modulate(0, 0, k, k == 0)
            for n in range(TT, len(pieces)):
                upper(n)
            turns(act, chunk)

        @block.vector
        def _(dve):
            def lower_a(i, b, k):
                g = TT * (2 * i + b) + k
                dve.wait_ge(a_hi_done, g + 1)
                nc.vector.tensor_tensor(a_lo[k % 2][:, :, :], a32[k % 2][:, :, :], a_hi[:, :, :].bitcast(F32), ALU.subtract).then_inc(a_lo_done, 1)

            def residual(i, b, k):
                g = TT * (2 * i + b) + k
                dve.wait_ge(proj_full, g + 1)
                dve.wait_ge(turned, g)
                nc.vector.tensor_tensor(proj[:, :], proj_ps[:, :], t.gates[:, 0, b, :], ALU.mult).then_inc(gated, 1)
                dve.wait_ge(gated, g + 1)
                dve.wait_ge(x_loaded[k % 2], 16 * (2 * (2 * i + b) + k // 2) + 16)
                nc.vector.tensor_tensor(xt[k % 2][:, :], proj[:, :], xt[k % 2][:, :], ALU.add).then_inc(x1_done, 1)
                dve.wait_ge(x1_done, g + 1)
                nc.vector.bn_stats(stats[:, :], xt[k % 2][:, :]).then_inc(stats_done, 1)
                dve.wait_ge(stats_done, g + 1)
                nc.vector.tensor_copy(t.scrap[:, 8:10], t.cols[:, 0:2])
                nc.vector.bn_aggr(mv[:, :], stats[:, :]).then_inc(mv_done, 1)
                dve.wait_ge(mv_done, g + 1)
                nc.vector.tensor_scalar(var_eps[:, :], mv[:, 1:2], LN_EPS, None, ALU.add).then_inc(eps_done, 1)

            def normalise(i, b, k):
                g = TT * (2 * i + b) + k
                dve.wait_ge(rstd_done, g + 1)
                nc.vector.tensor_scalar(xn[:, :], xt[k % 2][:, :], mv[:, 0:1], rstd[:, 0:1], ALU.subtract, ALU.mult).then_inc(xn_done, 1)

            def split_h(i, b, k):
                g = TT * (2 * i + b) + k
                tok = slice(k * P, (k + 1) * P)
                dve.wait_ge(h32_done, g + 1)
                nc.vector.tensor_copy(hT_hi[b][:, :, tok], h32[:, :, :]).then_inc(hT_hi_done, 1)
                dve.wait_ge(hT_hi_done, g + 1)
                nc.vector.tensor_tensor(hT_lo[b][:, :, tok], h32[:, :, :], hT_hi[b][:, :, tok].bitcast(F32), ALU.subtract).then_inc(hT_done, 1)

            def split_g(c, f):
                dve.wait_ge(f_free, FT * c + f + 1 + 2)
                dve.wait_ge(g_free, FT * c + f + 1)
                nc.vector.tensor_copy(g_hi[f % GR][:, :], g32[f % 2][:, :]).then_inc(g_hi_done, 1)
                dve.wait_ge(g_hi_done, FT * c + f + 1)
                nc.vector.tensor_tensor(g_lo[f % GR][:, :], g32[f % 2][:, :], g_hi[f % GR][:, :].bitcast(F32), ALU.subtract).then_inc(g_done, 1)

            def epilogue(i, b):
                c = 2 * i + b
                for k in range(TT):
                    if k < TT - 1:
                        dve.wait_ge(acc_full, (TT - 1) * c + k + 1)
                    else:
                        dve.wait_ge(g_free, FT * (c + 1) + GR)
                    nc.vector.tensor_tensor(acc_ps[k][:, :], acc_ps[k][:, :], t.gates[:, 1, b, :], ALU.mult).then_inc(acc_scaled, 1)
                    dve.wait_ge(acc_scaled, TT * c + k + 1)
                    dve.wait_ge(res_loaded[k], 16 * c + 16)
                    nc.vector.tensor_tensor(res[k][:, :], acc_ps[k][:, :], res[k][:, :], ALU.add).then_inc(acc_free, 1)

            def chunk(i, b, more, first):
                c = 2 * i + b
                for f in range(FT):
                    if more and f % 4 == 0:
                        lower_a(*nxt(i, b), f // 4)
                    split_g(c, f)
                    if f == 0 and not first:
                        epilogue(*prv(i, b))
                    if more and f % 4 == 1:
                        residual(*nxt(i, b), f // 4)
                    if more and f % 4 == 2:
                        split_h(*nxt(i, b), f // 4)
                    if more and f % 4 == 1:
                        normalise(*nxt(i, b), f // 4)

            for free, (sem_, n) in enumerate(((f_free, 2), (g_done, 2), (g_free, GR), (acc_free, TT))):
                nc.vector.memset(t.scrap[:, free:free + 1], 0.0).then_inc(sem_, n)
            def lower(n):
                dve.wait_ge(w_hi_done, n + 1)
                _, raw, hi, lo = pieces[n]
                nc.vector.tensor_tensor(lo, raw, hi.bitcast(F32), ALU.subtract).then_inc(w_lo_done, 1)

            nc.vector.memset(bias_rows[:, :].bitcast(F32), 0.0).then_inc(rows_set, 1)
            nc.vector.memset(pick_rows[:, :, :].bitcast(F32), 0.0).then_inc(rows_set, 1)
            dve.wait_ge(rows_set, 2)
            nc.vector.memset(pick_rows[0:33, 0, :].bitcast(F32), 1.0).then_inc(rows_set, 1)
            nc.vector.memset(pick_rows[64:97, 1, :].bitcast(F32), 1.0).then_inc(rows_set, 1)
            dve.wait_ge(brow_loaded, 32)
            for n in range(2):
                nc.vector.tensor_copy(bias_rows[64 * n:64 * n + 1, :], brow[n]).then_inc(brow_hi, 1)
            for n in range(2):
                dve.wait_ge(brow_hi, n + 1)
                nc.vector.tensor_tensor(bias_rows[64 * n + 32:64 * n + 33, :], brow[n], bias_rows[64 * n:64 * n + 1, :].bitcast(F32),
                                        ALU.subtract).then_inc(brow_lo, 1)
            dve.wait_ge(rows_set, 4)
            lower(0)
            lower_a(0, 0, 0)
            for k in range(TT):
                residual(0, 0, k)
                if k < TT - 1:
                    lower_a(0, 0, k + 1)
                normalise(0, 0, k)
                if k < TT - 1:
                    lower(k + 1)
                split_h(0, 0, k)
            for n in range(TT, len(pieces)):
                lower(n)
            turns(dve, chunk)
            epilogue(CPB - 1, 1)


class Shared:
    pass


def build(nc, ins, out):
    t = Shared()
    with ExitStack() as ctx:
        def sb(name, shape, dt=F32):
            return ctx.enter_context(nc.sbuf_tensor(name, shape, dt))

        t.qk_dram = nc.dram_tensor("qk_dram", [2, 2, NG, P, B, L], F32)
        t.v_dram = nc.dram_tensor("v_dram", [B, L, D], F32)
        t.rec_dram = nc.dram_tensor("rec_dram", [HG, CH], F32)
        t.a_dram = nc.dram_tensor("a_dram", [NG, P, B, L], F32)
        t.x1_dram = nc.dram_tensor("x1_dram", [B, L, D], F32)
        t.ident = sb("ident", [P, P])
        t.ones = sb("ones", [P, HD])
        t.minus_half = sb("minus_half", [P, 1])
        t.scrap = sb("scrap", [P, 10])
        t.cols = sb("cols", [P, N_ROWS])
        t.mod_w = sb("mod_w", [P, 2, B, KT])
        t.mod_b = sb("mod_b", [P, 2, B, KT])
        t.gates = sb("gates", [P, 2, B, D])
        with ExitStack() as early:
            t.wqkv_hi = early.enter_context(nc.sbuf_tensor("wqkv_hi", [P, KT, 3 * D], F32R))
            t.wqkv_raw, t.wqkv_lo = lower_half(nc, early, "wqkv_lo", [P, KT, 3 * D])
            t.v_bias = early.enter_context(nc.sbuf_tensor("v_bias", [P, D], F32))
            build_qkv(nc, t, ins)
        build_attention(nc, t)
        build_mlp(nc, t, ins, out)


_SHORT = {"x": "x", "cond_1024": "cond"} | {f"L0_cond_{n}": n for n in (
    "ln1_w", "ln1_b", "ln2_w", "ln2_b", "ada_w", "ada_b", "qkv_w", "qkv_b", "proj_w", "proj_b",
    "fc1_w", "fc1_b", "fc2_w", "fc2_b")}


def kernel(**inputs):
    import concourse.bacc as bacc
    from concourse.bass_utils import run_bass_kernel_spmd

    nc = bacc.Bacc("TRN2", target_bir_lowering=False, num_devices=1, dynamic_dma_scratch_size=1024)
    arrays, ins = {}, {}
    for name, short in _SHORT.items():
        a = np.ascontiguousarray(inputs[name])
        arrays[f"in_{short}"] = a
        ins[short] = nc.dram_tensor(f"in_{short}", a.shape, mybir.dt.from_np(a.dtype), kind="ExternalInput").ap()
    out = nc.dram_tensor("out_0", (B, L, D), F32, kind="ExternalOutput").ap()
    build(nc, ins, out)
    r = run_bass_kernel_spmd(nc, [arrays], core_ids=[0])
    return r.results[0]["out_0"]
```
